# Optimizing a Trainium2 kernel written in Bass

```python
import numpy as np
import jax
import jax.numpy as jnp

def _softmax(x, axis=-1):
    return jax.nn.softmax(x, axis=axis)

def _gelu(x):
    return jax.nn.gelu(x, approximate=True)

def _silu(x):
    return jax.nn.silu(x)

def _sigmoid(x):
    return jax.nn.sigmoid(x)

def _layernorm(x, axis=-1, eps=1e-05):
    m = jnp.mean(x, axis=axis, keepdims=True)
    v = jnp.var(x, axis=axis, keepdims=True)
    return (x - m) / jnp.sqrt(v + eps)

def _scatter_add(tgt, idx, src, axis=0):
    return tgt.at[idx].add(src)

def _segment_sum(src, seg, n):
    return jax.ops.segment_sum(src, seg, n)
kernel_name = 'mk_adj_ffn_d1_adj_r2_cd6fce'

def setup_inputs(seed: int=0):
    np.random.seed(seed)
    _w = jnp.asarray

    def _rec_inputs():
        import jax
        import jax.numpy as jnp
        _gk = jax.random.key(seed)
        x = -0.0005207 + 1.001 * jax.random.normal(jax.random.fold_in(_gk, 1), (1354, 128), jnp.float32)
        _a = jax.random.bernoulli(jax.random.fold_in(_gk, 2), 0.0118168, (1354, 1354))
        adj = _a.astype(jnp.int32)
        return (x, adj)
    x, adj = _rec_inputs()

    def _L0_gnn_setup():
        import jax, jax.numpy as jnp
        import numpy as np
        NEG_INF = -9000000000000000.0
        key = jax.random.key(seed)
        k1, k2, k3 = jax.random.split(key, 3)
        N, D = (4096, 128)
        h = jax.random.normal(k1, (N, D), dtype=jnp.float32)
        adj = jax.random.randint(k2, (N, N), 0, 2, dtype=jnp.int32)
        a = jax.random.normal(k3, (2 * D, 1), dtype=jnp.float32) * 0.1
        return {'h': h, 'adj': adj, 'a': a}
    _L0_gnn_all = _L0_gnn_setup()
    _L0_gnn_in = {k: v for k, v in _L0_gnn_all.items() if k in ('a',)}
    del _L0_gnn_all

    def _L0_ffn_setup():
        import jax, jax.numpy as jnp
        import numpy as np
        D_IN, D_HID, D_OUT = (128, 256, 128)
        N_EXPERTS, TOP_K = (64, 2)
        B, S = (8, 2048)
        key = jax.random.key(seed)
        ks = jax.random.split(key, 8)
        scale_in = 1.0 / np.sqrt(D_IN)
        scale_hid = 1.0 / np.sqrt(D_HID)
        return {'x': jax.random.normal(ks[0], (B, S, D_IN), dtype=jnp.float32), 'Wr': jax.random.uniform(ks[1], (D_IN, N_EXPERTS), jnp.float32, -scale_in, scale_in), 'br': jax.random.uniform(ks[2], (N_EXPERTS,), jnp.float32, -scale_in, scale_in), 'W1': jax.random.uniform(ks[3], (N_EXPERTS, D_IN, D_HID), jnp.float32, -scale_in, scale_in), 'b1': jax.random.uniform(ks[4], (N_EXPERTS, D_HID), jnp.float32, -scale_in, scale_in), 'W2': jax.random.uniform(ks[5], (N_EXPERTS, D_HID, D_OUT), jnp.float32, -scale_hid, scale_hid), 'b2': jax.random.uniform(ks[6], (N_EXPERTS, D_OUT), jnp.float32, -scale_hid, scale_hid)}
    _L0_ffn_all = _L0_ffn_setup()
    _L0_ffn_in = {k: v for k, v in _L0_ffn_all.items() if k in ('Wr', 'br', 'W1', 'b1', 'W2', 'b2')}
    del _L0_ffn_all
    return {'x': x, 'adj': adj, 'L0_gnn_a': _L0_gnn_in['a'], 'L0_ffn_Wr': _L0_ffn_in['Wr'], 'L0_ffn_br': _L0_ffn_in['br'], 'L0_ffn_W1': _L0_ffn_in['W1'], 'L0_ffn_b1': _L0_ffn_in['b1'], 'L0_ffn_W2': _L0_ffn_in['W2'], 'L0_ffn_b2': _L0_ffn_in['b2']}

def reference(x, adj, L0_gnn_a, L0_ffn_Wr, L0_ffn_br, L0_ffn_W1, L0_ffn_b1, L0_ffn_W2, L0_ffn_b2):
    import jax
    import jax.numpy as jnp

    def _L0_gnn_ref(h, adj, a):
        import jax, jax.numpy as jnp
        import numpy as np
        NEG_INF = -9000000000000000.0
        D = h.shape[1]
        alpha = 0.2
        wh1 = h @ a[:D, :]
        wh2 = h @ a[D:, :]
        e = jax.nn.leaky_relu(wh1 + wh2.T, negative_slope=alpha)
        att = jnp.where(adj > 0, e, NEG_INF)
        att = jax.nn.softmax(att, axis=1)
        h_prime = att @ h
        return h_prime

    def _L0_ffn_ref(x, Wr, br, W1, b1, W2, b2):
        import jax, jax.numpy as jnp
        import numpy as np
        D_IN, D_HID, D_OUT = (128, 256, 128)
        N_EXPERTS, TOP_K = (64, 2)
        B, S = (8, 2048)
        Bx, Sx, D = x.shape
        xf = x.reshape(-1, D)
        T = xf.shape[0]
        E = Wr.shape[1]
        logits = xf @ Wr + br
        topk_logits, topk_idx = jax.lax.top_k(logits, TOP_K)
        gates = jax.nn.softmax(topk_logits, axis=1)
        combine = jnp.zeros((T, E), xf.dtype).at[jnp.arange(T)[:, None], topk_idx].add(gates)
        out = jnp.zeros((T, W2.shape[-1]), xf.dtype)
        for e in range(E):
            h = jax.nn.relu(xf @ W1[e] + b1[e])
            y = h @ W2[e] + b2[e]
            out = out + combine[:, e:e + 1] * y
        return out.reshape(Bx, Sx, -1)
    x = x + _L0_gnn_ref(_layernorm(x, axis=-1), adj, L0_gnn_a)
    x = x + _L0_ffn_ref(_layernorm(x, axis=-1)[None], L0_ffn_Wr, L0_ffn_br, L0_ffn_W1, L0_ffn_b1, L0_ffn_W2, L0_ffn_b2)[0]
    return x

_drawn_inputs = setup_inputs


def setup_inputs(seed=0):
    import zlib

    import numpy as np

    out = dict(_drawn_inputs(seed))
    spreads = {}
    factors = {'L0_ffn_b1': 4.105}
    for name, (base, spread) in spreads.items():
        noise = np.random.default_rng([zlib.crc32(name.encode()), seed]).standard_normal(out[name].shape)
        drawn = base * np.exp(spread * noise) if base else spread * noise
        out[name] = jnp.asarray(drawn.astype(out[name].dtype))
    for name, factor in factors.items():
        out[name] = (out[name] * factor).astype(out[name].dtype)
    return out
```

```python
from contextlib import ExitStack

import concourse.bass as bass
from concourse import mybir

F32 = mybir.dt.float32
BF16 = mybir.dt.bfloat16
I32 = mybir.dt.int32
U32 = mybir.dt.uint32
ALU = mybir.AluOpType
ACT = mybir.ActivationFunctionType
AX_X = mybir.AxisListType.X

P = 128
BANK = 512
BIG = 2.0 ** 53
ALPHA = 0.2
EPS = 1e-5
CAP = 96
UNROLL = 16
PAIRS = UNROLL // 2
GSLOTS = 8


class Steps:

    def __init__(self, eng, sem):
        self.eng, self.sem, self.n = eng, sem, 0

    def clear(self):
        self.eng.sem_clear(self.sem)
        self.n = 0

    def link(self, ins):
        self.n += 1
        ins.then_inc(self.sem, 1)
        self.eng.wait_ge(self.sem, self.n)


def gat_moe(nc, x, adj, a, Wr, br, W1, b1, W2, b2, out):
    N, D = x.shape
    E, _, H = W1.shape
    HC = H // P
    NT = -(-N // P)
    LAST = N - P * (NT - 1)
    NP = NT * P
    ROUNDS = -(-N // CAP)
    ITERS = E // UNROLL
    NCH = -(-NP // BANK)
    TPC = BANK // P
    assert D == P and H == 2 * P and NT % 2 == 1 and E % UNROLL == 0 and NCH == 3

    ctx = ExitStack()
    with ctx:
        def sb(name, shape, dt=F32):
            return ctx.enter_context(nc.sbuf_tensor(name, shape, dt))

        def sem(name):
            return ctx.enter_context(nc.semaphore(name))

        banks = [ctx.enter_context(nc.psum_tensor(f"bank{i}", [P, BANK], F32)) for i in range(8)]
        s_bank, z_bank, o_bank = banks[0:2], banks[2:4], banks[4:6]
        rp_bank, c_bank = banks[6], banks[7]
        x_bank, h_bank, y_bank = banks[0:2], banks[2:4], banks[4:6]

        xh2_dram = nc.dram_tensor("xh2_rows", [N, D], F32, kind="Internal").ap()
        y_dram = nc.dram_tensor("expert_rows", [ROUNDS * E * CAP, D], F32, kind="Internal").ap()

        x_sb = sb("x_sb", [P, NT, D])
        a_sb = sb("a_sb", [P, 2])
        Wr_sb = sb("Wr_sb", [P, E])
        br_bc = sb("br_bc", [P, E])
        b1_sb = sb("b1_sb", [E, H])
        b2_sb = sb("b2_sb", [E, D])
        identf = sb("identf", [P, P])
        identb = sb("identb", [P, P], BF16)
        before = sb("before", [P, P], BF16)
        ones_bf = sb("ones_bf", [P, P], BF16)
        ones_f = sb("ones_f", [P, P])
        iota_e = sb("iota_e", [P, E])
        iota_r = sb("iota_r", [P, CAP])
        row_of_e = sb("row_of_e", [P, NT, E])
        tok_lo = sb("tok_lo", [P, 1])
        tile_base = sb("tile_base", [P, NT, E], BF16)
        neg_half = sb("neg_half", [P, NT])
        bn = sb("bn", [P, NT, 6])
        mv = sb("mv", [P, NT, 2])
        ve = sb("ve", [P, NT])
        rstd = sb("rstd", [P, NT])
        hx = sb("hx", [P, NT, D + 1])
        hT = sb("hT", [P, NP])
        a2_bc = sb("a2_bc", [P, P])
        w2_bc = sb("w2_bc", [P, NP])
        w3 = sb("w3", [P, NT, 3])
        w1_col = sb("w1_col", [P, NT])
        aw1_col = sb("aw1_col", [P, NT])
        w3r = sb("w3r", [P, NT, 3])
        w3q = sb("w3q", [P, NT, 3])
        parts = sb("parts", [P, NT, 18], BF16)
        L = sb("L", [P, NP], BF16)
        RS = sb("RS", [P, NP], BF16)
        RP = sb("RP", [P, 2, P], BF16)
        hsum = sb("hsum", [P, D + 1])
        adj_sb = sb("adj_sb", [P, 2, N], I32)
        nmask = sb("nmask", [P, 2, NP], BF16)
        junk = sb("junk", [P, 2, N], BF16)
        rmax = sb("rmax", [P, 2])
        chain_a = sb("chain_a", [P, 2, 6])
        vparts = sb("vparts", [P, 2, 9], BF16)
        alone = sb("alone", [P, NT])
        relu_s = sb("relu_s", [P, 2, BANK])
        z_sb = sb("z_sb", [P, 2, BANK])
        p_sb = sb("p_sb", [P, 2, NT, P])
        o_sb = sb("o_sb", [P, 2, D + 1])
        rden = sb("rden", [P, 2])
        x1 = sb("x1", [P, NT, D])
        bn2 = sb("bn2", [P, 2, 6])
        mv2 = sb("mv2", [P, 2, 2])
        ve2 = sb("ve2", [P, 2])
        rstd2 = sb("rstd2", [P, 2])
        xh2 = sb("xh2", [P, 2, D])
        xh2T = sb("xh2T", [P, 2, P])
        logit = sb("logit", [P, 2, E])
        top8 = sb("top8", [P, 2, 8])
        idx8 = sb("idx8", [P, 2, 8], U32)
        top2 = sb("top2", [P, NT, 2])
        exp2 = sb("exp2", [P, 2, NT])
        oh = sb("oh", [P, 2, NT, E], BF16)
        ohcum = sb("ohcum", [P, NT + 1, E], BF16)
        ohsum = sb("ohsum", [P, 2, E], BF16)
        rowno = sb("rowno", [P, NT, E])
        picked = sb("picked", [P, 2, NT, E])
        ypos = sb("ypos", [P, 2, NT])
        ypos_i = sb("ypos_i", [P, 2, NT], I32)
        rank = sb("rank", [P, 2, NT])
        later = sb("later", [P, 2, NT])
        oh_lo = sb("oh_lo", [P, 2, NT, E], BF16)
        oh_hi = sb("oh_hi", [P, 2, NT, E], BF16)
        rank_oh = sb("rank_oh", [P, 2, NT, CAP], BF16)
        cnt = sb("cnt", [P, 1])
        cnt_i = sb("cnt_i", [P, 1], I32)
        tok_i = sb("tok_i", [CAP, E], I32)
        ge = sb("ge", [P, NT])
        gden = sb("gden", [P, NT])
        g1 = sb("g1", [P, NT])
        g2 = sb("g2", [P, NT])
        gmat = sb("gmat", [P, NT, E])
        gmat2 = sb("gmat2", [P, NT, E])
        gT = sb("gT", [E, NP])
        tok_now = sb("tok_now", [CAP, 2, GSLOTS], I32)
        xg = sb("xg", [CAP, GSLOTS, D])
        xT = sb("xT", [P, 2, CAP])
        w1_ring = sb("w1_ring", [P, UNROLL, H])
        w2_ring = sb("w2_ring", [P, UNROLL, HC, D])
        b1T = sb("b1T", [P, HC, E])
        hidden = sb("hidden", [P, 2, HC, CAP])
        y_sb = sb("y_sb", [CAP, 4, 2, D])
        yg = hT[:, 0:8 * D].rearrange("p (s d) -> p s d", s=8)

        x_in = sem("x_in")
        xl_in = sem("xl_in")
        small_in = sem("small_in")
        adj_in = [sem(f"adj_in{i}") for i in range(2)]
        adj_last_in = sem("adj_last_in")
        stats_ready = sem("stats_ready")
        rstd_ready = sem("rstd_ready")
        h_ready = sem("h_ready")
        hT_ps = sem("hT_ps")
        hT_ready = sem("hT_ready")
        w_ps = sem("w_ps")
        w2bc_ps = sem("w2bc_ps")
        w2bc_ready = sem("w2bc_ready")
        parts_ready = sem("parts_ready")
        partsT_ps = sem("partsT_ps")
        L_ready = sem("L_ready")
        a2_ready = sem("a2_ready")
        hsum_ps = sem("hsum_ps")
        b1T_ps = sem("b1T_ps")
        hsum_ready = sem("hsum_ready")
        mask_ready = sem("mask_ready")
        rowmax_ready = sem("rowmax_ready")
        v_ready = sem("v_ready")
        vT_ps = sem("vT_ps")
        RP_ready = sem("RP_ready")
        s_ps = sem("s_ps")
        relu_ready = sem("relu_ready")
        z_ps = sem("z_ps")
        z_ready = sem("z_ready")
        p_ready = sem("p_ready")
        o_ps = sem("o_ps")
        xh2_ready = sem("xh2_ready")
        xh2T_ps = sem("xh2T_ps")
        xh2T_ready = sem("xh2T_ready")
        logit_ps = sem("logit_ps")
        logit_ready = sem("logit_ready")
        oh_ready = sem("oh_ready")
        ohcum_ready = sem("ohcum_ready")
        xh2_out = [sem(f"xh2_out{i}") for i in range(2)]
        dve_step = sem("dve_step")
        mv2_ready = sem("mv2_ready")
        rstd2_ready = sem("rstd2_ready")
        pool_step = sem("pool_step")
        rank_ps = sem("rank_ps")
        diff_ready = sem("diff_ready")
        gexp_ready = sem("gexp_ready")
        rank_oh_ready = sem("rank_oh_ready")
        rank_ready = sem("rank_ready")
        later_ready = sem("later_ready")
        stores_landed = sem("stores_landed")
        tok_ps = sem("tok_ps")
        tok_ready = sem("tok_ready")
        count_ready = sem("count_ready")
        ypos_ready = sem("ypos_ready")
        gmat_ready = sem("gmat_ready")
        tok_now_ready = sem("tok_now_ready")
        xg_in = [sem(f"xg_in{i}") for i in range(GSLOTS)]
        w_in = [sem(f"w_in{i}") for i in range(PAIRS)]
        xT_ps = sem("xT_ps")
        xT_ready = sem("xT_ready")
        h_ps = sem("h_ps")
        hid_ready = sem("hid_ready")
        y_ps = sem("y_ps")
        y_ready = sem("y_ready")
        y_out = [sem(f"y_out{i}") for i in range(4)]
        gT_ps = sem("gT_ps")
        gT_ready = sem("gT_ready")
        bias_ps = sem("bias_ps")
        bias_done = sem("bias_done")
        yg_in = [sem(f"yg_in{i}") for i in range(8)]
        row_done = sem("row_done")
        out_written = sem("out_written")
        dve_link = sem("dve_link")
        pool_link = sem("pool_link")
        const_made = sem("const_made")
        passed = sem("passed")

        LOADS = 5
        STEADY0, STEADY1 = 4, 8
        rows_of = lambda t: P if isinstance(t, int) and t < NT - 1 or not isinstance(t, int) else LAST

        def chunk_tiles(c):
            return list(range(c * TPC, min((c + 1) * TPC, NT)))

        def attention_steps(eng, step, steps=None):
            for t in range(-1, STEADY0):
                step(t, t % 2)
            with eng.Fori(STEADY0 // 2, STEADY1 // 2) as i:
                if steps:
                    steps.clear()
                step(i * 2, 0)
                step(i * 2 + 1, 1)
            if steps:
                steps.clear()
            for t in range(STEADY1, NT + 2):
                step(t, t % 2)

        def stages(t):
            if not isinstance(t, int):
                return True, True, True, True
            return t + 1 < NT, 0 <= t < NT, 0 <= t - 1 < NT, 0 <= t - 2 < NT

        def wait_apart(eng, semaphore, value):
            eng.wait_ge(semaphore, value)
            if not isinstance(value, int):
                eng.sem_inc(passed, 1)

        def tiles3(buf, k, n):
            return buf[:, 0:k * P].rearrange("p (t c) -> p t c", c=P)[:, :, 0:n]

        def loads16(u, q):
            return (u - q) * 8 + 16

        CONST = 9
        PARTS_AT = ((0, 0, 0, 0, 8), (0, 1, 0, 8, NT - 8), (1, 2, 0, 0, 8), (1, 1, NT - 8, 8, NT - 8))

        def expert_rounds(eng, step):
            def one(rnd, first):
                for e in range(UNROLL):
                    step(rnd, e, e, None, first)
                with eng.Fori(1, ITERS) as it:
                    for k in range(UNROLL):
                        step(rnd, it * UNROLL + k, k, it, first)
                for e in (E, E + 1):
                    step(rnd, e, e - E, None, first)
            one(0, True)
            most = most_tokens(eng)
            with eng.If(most > CAP):
                with eng.Fori(1, ROUNDS) as rnd:
                    one(rnd, False)

        def most_tokens(eng):
            eng.wait_ge(count_ready, 1)
            return eng.value_load(cnt_i[0:1, 0:1], min_val=0, max_val=N)

        def nth_use(slots, back, e, k, it):
            if isinstance(e, int):
                return (e - back) // slots + 1
            return it * (UNROLL // slots) + (k - back) // slots + 1

        block = ctx.enter_context(nc.Block())

        @block.sync
        def _(sp):
            sp.dma_start(x_sb[:, 0:NT - 1, :], x[0:P * (NT - 1), :].rearrange("(t p) d -> p t d", p=P)).then_inc(x_in, 16)
            sp.dma_start(x_sb[0:LAST, NT - 1, :], x[P * (NT - 1):N, :]).then_inc(xl_in, 16)
            sp.dma_start(adj_sb[:, 0, :], adj[0:P, :]).then_inc(adj_in[0], 16)
            sp.dma_start(adj_sb[:, 1, :], adj[P:2 * P, :]).then_inc(adj_in[1], 16)

            def load_weights(it, pair, e0):
                sp.dma_start(w1_ring[:, 2 * pair:2 * pair + 2, :],
                             W1[bass.ds(e0, 2), :, :].rearrange("e p h -> p e h")).then_inc(w_in[pair], 16)
                sp.dma_start(w2_ring[:, 2 * pair:2 * pair + 2, :, :].rearrange("p e c d -> p (e c) d"),
                             W2[bass.ds(e0, 2), :, :].rearrange("e (c p) d -> p (e c) d", p=P)).then_inc(w_in[pair], 16)

            def step(t, par):
                _, has_b, has_c1, _ = stages(t)
                if not isinstance(t, int) or 0 <= t < NT - 3:
                    sp.wait_ge(mask_ready, t + 1)
                    sp.dma_start(adj_sb[:, par, :], adj[bass.ds((t + 2) * P, P), :]).then_inc(adj_in[par], 16)
                if isinstance(t, int) and t == NT - 3:
                    sp.wait_ge(mask_ready, t + 1)
                    sp.dma_start(adj_sb[0:LAST, par, :], adj[(NT - 1) * P:N, :]).then_inc(adj_in[par], 16)
                    for k in range(PAIRS):
                        load_weights(0, k, 2 * k)
                if has_c1:
                    sp.wait_ge(xh2_ready, t)
                    n = rows_of(t - 1)
                    q = (par + 1) % 2
                    sp.dma_start(xh2_dram[bass.ds((t - 1) * P, n), :], xh2[0:n, q, :]).then_inc(xh2_out[q], 16)

            attention_steps(sp, step)

            def weights_round(rnd):
                with sp.Fori(0, ITERS - 1) as it:
                    for k in range(PAIRS):
                        sp.wait_ge(y_ps, rnd * E + it * UNROLL + 2 * k + 2)
                        load_weights(None, k, (it + 1) * UNROLL + 2 * k)

            weights_round(0)
            most = most_tokens(sp)
            with sp.If(most > CAP):
                with sp.Fori(1, ROUNDS) as rnd:
                    for k in range(PAIRS):
                        sp.wait_ge(y_ps, rnd * E - UNROLL + 2 * k + 2)
                        load_weights(None, k, 2 * k)
                    weights_round(rnd)
            for t in range(NT):
                sp.wait_ge(row_done, t + 1)
                n = rows_of(t)
                sp.dma_start(out[t * P:t * P + n, :], x1[0:n, t, :]).then_inc(out_written, 16)
            sp.wait_ge(out_written, 16 * NT)

        @block.gpsimd
        def _(pool):
            pool.memset(identf[:, :], 0.0).then_inc(pool_step, 1)
            pool.memset(ones_f[:, :], 1.0).then_inc(pool_step, 1)
            pool.memset(identb[:, :], 0.0).then_inc(pool_step, 1)
            pool.memset(ones_bf[:, :], 1.0).then_inc(pool_step, 1)
            pool.memset(neg_half[:, :], -0.5).then_inc(pool_step, 1)
            pool.wait_ge(pool_step, 5)
            for ident in (identf, identb):
                pool.affine_select(out=ident[:, :], in_=ident[:, :], compare_op=ALU.not_equal, fill=1.0, base=0,
                                   pattern=[[-1, P]], channel_multiplier=1).then_inc(pool_step, 1)
            pool.affine_select(out=before[:, :], in_=ones_bf[:, :], compare_op=ALU.is_gt, fill=0.0, base=0,
                               pattern=[[1, P]], channel_multiplier=-1).then_inc(pool_step, 1)
            pool.iota(iota_e[:, :], [[1, E]], base=0, channel_multiplier=0,
                      allow_small_or_imprecise_dtypes=True).then_inc(pool_step, 1)
            pool.iota(iota_r[:, :], [[1, CAP]], base=0, channel_multiplier=0,
                      allow_small_or_imprecise_dtypes=True).then_inc(pool_step, 1)
            pool.iota(row_of_e[:, :, :], [[0, NT], [CAP, E]], base=0, channel_multiplier=0,
                      allow_small_or_imprecise_dtypes=True).then_inc(pool_step, 1)
            pool.iota(tok_lo[:, :], [[0, 1]], base=0, channel_multiplier=1,
                      allow_small_or_imprecise_dtypes=True).then_inc(pool_step, 1)
            pool.iota(tile_base[:, :, :], [[P, NT], [0, E]], base=0, channel_multiplier=0,
                      allow_small_or_imprecise_dtypes=True).then_inc(pool_step, 1)
            pool.wait_ge(pool_step, 13)
            pool.memset(L[:, :], 0.0).then_inc(const_made, 1)
            pool.memset(RS[:, :], 0.0).then_inc(const_made, 1)
            pool.memset(RP[:, :, :], 0.0).then_inc(const_made, 1)
            pool.memset(vparts[:, :, 0:3], 0.0).then_inc(const_made, 1)
            pool.memset(vparts[:, :, 3:6], 1.0).then_inc(const_made, 1)
            pool.memset(oh[:, :, NT - 1, :], 0.0).then_inc(const_made, 1)
            pool.memset(exp2[:, :, NT - 1], 0.0).then_inc(const_made, 1)
            pool.memset(top2[:, NT - 1, :], 0.0).then_inc(const_made, 1)
            pool.memset(ohcum[:, 0, :], 0.0).then_inc(const_made, 1)
            CONST = 9
            pool.wait_ge(stats_ready, 1)
            pool.tensor_scalar(ve[:, :], mv[:, :, 1], EPS, None, ALU.add).then_inc(pool_step, 1)
            pool.wait_ge(pool_step, 14)
            pool.tensor_tensor(rstd[:, :], ve[:, :], neg_half[:, :], ALU.pow).then_inc(rstd_ready, 1)
            pool.wait_ge(rstd_ready, 1)
            pool.wait_ge(const_made, CONST)

            steps = Steps(pool, pool_link)
            link = steps.link

            def col(buf, t):
                return buf[:, t:t + 1] if isinstance(t, int) else buf[:, bass.ds(t, 1)]

            def step(t, par):
                has_a, _, has_c1, has_c2 = stages(t)
                if has_c1:
                    q = (par + 1) % 2
                    n = rows_of(t - 1)
                    wait_apart(pool, mv2_ready, t)
                    link(pool.tensor_scalar(ve2[0:n, q:q + 1], mv2[0:n, q, 1:2], EPS, None, ALU.add))
                    pool.tensor_tensor(rstd2[0:n, q:q + 1], ve2[0:n, q:q + 1], neg_half[0:n, 0:1],
                                       ALU.pow).then_inc(rstd2_ready, 1)
                if has_a:
                    q = (par + 1) % 2
                    n = rows_of(t + 1)
                    c = chain_a
                    w1, aw1 = (b[0:n, t + 1:t + 2] if isinstance(t, int) else b[:, bass.ds(t + 1, 1)] for b in (w1_col, aw1_col))
                    pool.wait_ge(rowmax_ready, t + 2)
                    link(pool.tensor_tensor(c[0:n, q, 0:1], rmax[0:n, q:q + 1], w1, ALU.add))
                    link(pool.tensor_scalar(c[0:n, q, 1:2], c[0:n, q, 0:1], ALPHA, c[0:n, q, 0:1], ALU.mult, ALU.max))
                    link(pool.tensor_tensor(c[0:n, q, 2:3], aw1, c[0:n, q, 1:2], ALU.subtract))
                    if not isinstance(t, int) or t >= 1:
                        pool.wait_ge(vT_ps, t)
                    link(pool.tensor_copy(vparts[0:n, q, 6:7], c[0:n, q, 2:3]))
                    link(pool.tensor_tensor(c[0:n, q, 3:4], c[0:n, q, 2:3], vparts[0:n, q, 6:7], ALU.subtract))
                    link(pool.tensor_copy(vparts[0:n, q, 7:8], c[0:n, q, 3:4]))
                    pool.tensor_tensor(vparts[0:n, q, 8:9], c[0:n, q, 3:4], vparts[0:n, q, 7:8],
                                       ALU.subtract).then_inc(v_ready, 1)
                if has_c2:
                    t2 = t - 2
                    def tile_e(buf, k, u):
                        if k is None:
                            return buf[:, u, :] if isinstance(t, int) else buf[:, bass.ds(u, 1), :].rearrange("p o e -> p (o e)")
                        return buf[:, k, u, :] if isinstance(t, int) else buf[:, k, bass.ds(u, 1), :].rearrange("p o e -> p (o e)")
                    pool.wait_ge(oh_ready, t2 + 1)
                    link(pool.tensor_tensor(ohsum[:, par, :], tile_e(oh, 0, t2), tile_e(oh, 1, t2), ALU.add))
                    if not isinstance(t, int) or t2 >= 1:
                        pool.wait_ge(ohcum_ready, t2)
                    pool.tensor_tensor(tile_e(ohcum, None, t2 + 1), tile_e(ohcum, None, t2), ohsum[:, par, :],
                                       ALU.add).then_inc(ohcum_ready, 1)

            attention_steps(pool, step, steps)

            for par, k in ((0, (NT + 1) // 2), (1, NT // 2)):
                pool.wait_ge(xh2_out[par], 16 * k)

            def gathers(rnd):
                wait_apart(pool, tok_ready, rnd + 1)
                with pool.Fori(0, ITERS) as it:
                    for k in range(UNROLL):
                        half, s = k // GSLOTS, k % GSLOTS
                        if s == 0:
                            pool.tensor_copy(tok_now[:, half, :],
                                             tok_i[:, bass.ds(it * UNROLL + half * GSLOTS, GSLOTS)]).then_inc(tok_now_ready, 1)
                            pool.wait_ge(tok_now_ready, rnd * (E // GSLOTS) + it * 2 + half + 1)
                        wait_apart(pool, xT_ps, rnd * E + it * UNROLL + k + 1)
                        pool.indirect_dma_start(xg[:, s, :], None, xh2_dram,
                                                bass.IndirectOffsetOnAxis(ap=tok_now[:, half, s:s + 1], axis=0)
                                                ).then_inc(xg_in[s], 16)
                for k in range(4):
                    pool.wait_ge(y_out[k], 16 * (E // 8) * (rnd + 1))

            def combine(table, ready):
                pool.wait_ge(ypos_ready, ready)
                for t in range(NT):
                    for k in range(2):
                        n = 2 * t + k
                        if n >= 8:
                            pool.wait_ge(row_done, (n - 8) // 2 + 1)
                        pool.indirect_dma_start(yg[:, n % 8, :], None, table,
                                                bass.IndirectOffsetOnAxis(ap=ypos_i[:, k, t:t + 1], axis=0)
                                                ).then_inc(yg_in[n % 8], 16)

            gathers(0)
            most = most_tokens(pool)
            with pool.If(most > CAP):
                with pool.Fori(1, ROUNDS) as rnd:
                    gathers(rnd)
                combine(y_dram, 2)
            with pool.Else():
                combine(y_dram[0:E * CAP, :], 1)

        @block.scalar
        def _(act):
            act.dma_start(a_sb[:, :], a.rearrange("(c p) o -> p (c o)", p=P),
                          allow_slow_non_contiguous=True).then_inc(small_in, 16)
            act.dma_start(Wr_sb[:, :], Wr).then_inc(small_in, 16)
            act.dma_start(br_bc[:, :], br.unsqueeze(0).to_broadcast([P, E])).then_inc(small_in, 16)
            act.dma_start(b1_sb[:, :], b1).then_inc(small_in, 16)
            act.dma_start(b2_sb[:, :], b2).then_inc(small_in, 16)
            for c in range(NCH):
                w = min(BANK, NP - c * BANK)
                act.wait_ge(hT_ps, c + 1)
                act.copy(hT[:, c * BANK:c * BANK + w], banks[c][:, 0:w]).then_inc(hT_ready, 1)
            for c in range(NCH):
                w = min(BANK, NP - c * BANK)
                act.wait_ge(w2bc_ps, c + 1)
                act.copy(w2_bc[:, c * BANK:c * BANK + w], banks[3 + c][:, 0:w]).then_inc(w2bc_ready, 1)
            act.wait_ge(const_made, CONST)
            act.wait_ge(partsT_ps, 1)
            for dst, bank, off, t0, k in PARTS_AT:
                view = banks[bank][0:9, :].bitcast(BF16)
                act.copy((L, RS)[dst][0:9, t0 * P:(t0 + k) * P], view[:, off * P:(off + k) * P]).then_inc(L_ready, 1)
            act.wait_ge(hsum_ps, 1)
            act.copy(hsum[:, :], c_bank[:, 0:D + 1]).then_inc(hsum_ready, 1)
            act.wait_ge(b1T_ps, 1)
            act.copy(b1T[:, :, :], banks[4][:, 0:HC * E].rearrange("p (c e) -> p c e", c=HC)).then_inc(hsum_ready, 1)

            def step(t, par):
                has_a, has_b, _, has_c2 = stages(t)
                n = rows_of(t)

                def relu(c):
                    k = len(chunk_tiles(c))
                    act.wait_ge(s_ps, 3 * t + c + 1)
                    b = (par + c) % 2
                    act.activation(tiles3(relu_s[:, b, :], k, n), tiles3(s_bank[b], k, n), ACT.Relu,
                                   scale=1.0 - ALPHA).then_inc(relu_ready, 1)

                def exp(c):
                    k = len(chunk_tiles(c))
                    act.wait_ge(z_ready, 3 * t + c + 1)
                    b = (par + c) % 2
                    act.activation(p_sb[:, par, c * TPC:c * TPC + k, 0:n], tiles3(z_sb[:, b, :], k, n),
                                   ACT.Exp).then_inc(p_ready, 1)

                if has_b:
                    relu(0)
                    relu(1)
                    exp(0)
                    relu(2)
                if has_c2:
                    m = rows_of(t - 2)
                    act.wait_ge(xh2T_ps, t - 1)
                    act.copy(xh2T[:, par, 0:m], c_bank[:, 0:m]).then_inc(xh2T_ready, 1)
                if has_b:
                    exp(1)
                if has_a:
                    m = rows_of(t + 1)
                    act.wait_ge(vT_ps, t + 2)
                    act.copy(RP[0:9, (par + 1) % 2, 0:m], rp_bank[0:9, :].bitcast(BF16)[:, 0:m]).then_inc(RP_ready, 1)
                if has_b:
                    exp(2)

            attention_steps(act, step)
            act.wait_ge(diff_ready, 1)
            act.activation(ge[:, :], gden[:, :], ACT.Exp).then_inc(gexp_ready, 1)

            def step(rnd, e, k, it, first):
                if not isinstance(e, int) or e < E:
                    act.wait_ge(xT_ps, GSLOTS + rnd * E + e + 1)
                    act.copy(xT[:, k % 2, :], x_bank[k % 2][:, 0:CAP]).then_inc(xT_ready, 1)
                if not isinstance(e, int) or e >= 2:
                    q = (k - 2) % UNROLL // 2
                    u = (k - 2) % 2
                    if u == 0 and not (first and isinstance(e, int) and e - 2 < 8):
                        act.wait_ge(y_out[q % 4], 16 * (E // 8) * rnd + 16 * (nth_use(8, 2, e, k, it) - 1))
                    act.wait_ge(y_ps, rnd * E + e - 1)
                    act.copy(y_sb[:, q % 4, u, :], y_bank[k % 2][0:CAP, 0:D]).then_inc(y_ready, 1)
                    if u == 1:
                        act.wait_ge(y_ready, rnd * E + e - 1)
                        rows = y_dram.rearrange("(e r) d -> r e d", r=CAP)
                        act.dma_start(rows[:, bass.ds(rnd * E + e - 3, 2), :],
                                      y_sb[:, q % 4, :, :]).then_inc(y_out[q % 4], 16)

            expert_rounds(act, step)
            for c in range(NCH):
                w = min(BANK, NP - c * BANK)
                act.wait_ge(gT_ps, c + 1)
                act.copy(gT[:, c * BANK:c * BANK + w], rp_bank[0:E, 0:w]).then_inc(gT_ready, 1)

        @block.tensor
        def _(pe):
            pe.sem_inc(xT_ps, GSLOTS)
            pe.wait_ge(pool_step, 13)
            pe.wait_ge(h_ready, 1)
            for t in range(NT):
                last = pe.transpose(banks[t // TPC][:, t % TPC * P:(t % TPC + 1) * P], hx[:, t, 0:D], identf[:, :])
                if t % TPC == TPC - 1 or t == NT - 1:
                    last.then_inc(hT_ps, 1)
            pe.wait_ge(hT_ready, NCH)
            pe.wait_ge(small_in, 16 * LOADS)
            for t in range(NT):
                last = pe.matmul(rp_bank[:, 2 * t:2 * t + 2], hT[:, t * P:(t + 1) * P], a_sb[:, :], start=True, stop=True)
            last.then_inc(w_ps, 1)
            pe.wait_ge(a2_ready, 1)
            for c in range(NCH):
                w = min(BANK, NP - c * BANK)
                pe.matmul(banks[3 + c][:, 0:w], a2_bc[:, :], hT[:, c * BANK:c * BANK + w],
                          start=True, stop=True).then_inc(w2bc_ps, 1)
            pe.wait_ge(parts_ready, 1)
            for dst, bank, off, t0, k in PARTS_AT:
                view = banks[bank][0:9, :].bitcast(BF16)
                cols = slice(9, 18) if dst == 0 else slice(0, 9)
                for j in range(k):
                    last = pe.transpose(view[:, (off + j) * P:(off + j + 1) * P], parts[:, t0 + j, cols], identb[:, :])
            last.then_inc(partsT_ps, 1)

            def mask_parts(t, par):
                m = rows_of(t + 1)
                pe.wait_ge(v_ready, t + 2)
                if not isinstance(t, int) or t >= 0:
                    pe.wait_ge(RP_ready, t + 1)
                pe.transpose(rp_bank[0:9, :].bitcast(BF16)[:, 0:m], vparts[0:m, (par + 1) % 2, :],
                             identb[0:m, 0:m]).then_inc(vT_ps, 1)

            def step(t, par):
                has_a, has_b, has_c1, has_c2 = stages(t)
                n = rows_of(t)

                def sums(c):
                    b = (par + c) % 2
                    if not isinstance(t, int) or 3 * t + c >= 2:
                        pe.wait_ge(relu_ready, 3 * t + c - 1)
                    for j in chunk_tiles(c):
                        o = j % TPC * P
                        rs = RS[:, t * P:t * P + n] if isinstance(t, int) else RS[:, bass.ds(t * P, P)]
                        last = pe.matmul(s_bank[b][:, o:o + n], L[:, j * P:(j + 1) * P], rs, start=True, stop=True)
                    last.then_inc(s_ps, 1)

                def masked(c):
                    b = (par + c) % 2
                    if not isinstance(t, int) or 3 * t + c >= 2:
                        pe.wait_ge(z_ready, 3 * t + c - 1)
                    for j in chunk_tiles(c):
                        o = j % TPC * P
                        pe.matmul(z_bank[b][:, o:o + n], nmask[0:n, par, j * P:(j + 1) * P], identb[0:n, 0:n],
                                  start=True, stop=False)
                        last = pe.matmul(z_bank[b][:, o:o + n], L[:, j * P:(j + 1) * P], RP[:, par, 0:n],
                                         start=False, stop=True)
                    last.then_inc(z_ps, 1)

                def weigh(u, upar, c):
                    m = rows_of(u)
                    pe.wait_ge(p_ready, 3 * u + c + 1)
                    if c == 0 and (not isinstance(u, int) or u >= 2):
                        pe.wait_ge(mv2_ready, u - 1)
                    for j in chunk_tiles(c):
                        last = pe.matmul(o_bank[upar][0:m, 0:D + 1], p_sb[:, upar, j, 0:m], hx[:, j, :],
                                         start=(j == 0), stop=(j == NT - 1))
                    if c == NCH - 1:
                        last.then_inc(o_ps, 1)

                if has_b:
                    sums(0)
                    sums(1)
                    pe.wait_ge(RP_ready, t + 1)
                    pe.wait_ge(mask_ready, t + 1)
                    masked(0)
                    masked(1)
                if has_c1:
                    weigh(t - 1, (par + 1) % 2, 2)
                if has_b:
                    sums(2)
                    masked(2)
                if has_c2:
                    m = rows_of(t - 2)
                    pe.wait_ge(xh2_ready, t - 1)
                    if not isinstance(t, int) or t - 2 >= 1:
                        pe.wait_ge(logit_ready, t - 2)
                    pe.transpose(c_bank[:, 0:m], xh2[0:m, par, :], identf[0:m, 0:m]).then_inc(xh2T_ps, 1)
                if has_b:
                    weigh(t, par, 0)
                if has_c2:
                    m = rows_of(t - 2)
                    pe.wait_ge(xh2T_ready, t - 1)
                    pe.matmul(c_bank[0:m, 0:E], xh2T[:, par, 0:m], Wr_sb[:, :], start=True, stop=True).then_inc(logit_ps, 1)
                if has_a:
                    mask_parts(t, par)
                if has_b:
                    weigh(t, par, 1)
            pe.wait_ge(w2bc_ready, NCH)
            for j in range(NT):
                last = pe.matmul(c_bank[:, 0:D + 1], ones_f[:, :], hx[:, j, :], start=(j == 0), stop=(j == NT - 1))
            last.then_inc(hsum_ps, 1)
            for c in range(HC):
                last = pe.transpose(banks[4][:, c * E:(c + 1) * E], b1_sb[:, c * P:(c + 1) * P], identf[0:E, 0:E])
            last.then_inc(b1T_ps, 1)
            pe.wait_ge(L_ready, len(PARTS_AT))
            pe.wait_ge(hsum_ready, 2)

            attention_steps(pe, step)

            pe.wait_ge(ohcum_ready, NT)
            for bank, t0, t1 in ((banks[2], 0, 8), (banks[3], 8, NT)):
                w = (t1 - t0) * E
                pe.matmul(bank[:, 0:w], before[:, :], oh[:, 0, t0:t1, :], start=True, stop=False)
                pe.matmul(bank[:, 0:w], before[:, :], oh[:, 1, t0:t1, :], start=False, stop=False)
                pe.matmul(bank[:, 0:w], ones_bf[:, :], ohcum[:, t0:t1, :], start=False, stop=True)
            pe.matmul(banks[3][:, 3 * E:4 * E], ones_bf[:, :], ohcum[:, NT, :], start=True, stop=True).then_inc(rank_ps, 1)

            def lists(rnd):
                for k in range(2):
                    pe.wait_ge(rank_oh_ready, 2 * rnd + k + 1)
                    for t in range(NT):
                        for v, buf in enumerate((oh_lo, oh_hi)):
                            last = pe.matmul(c_bank[0:CAP, 0:E], rank_oh[:, k, t, :], buf[:, k, t, :],
                                             start=(k == 0 and t == 0 and v == 0), stop=(k == 1 and t == NT - 1 and v == 1))
                last.then_inc(tok_ps, 1)

            def step(rnd, e, k, it, first):
                if isinstance(e, int) and e == 0:
                    lists(rnd)
                if not isinstance(e, int) or e < E:
                    pe.wait_ge(xg_in[k % GSLOTS], 16 * (E // GSLOTS) * rnd + 16 * nth_use(GSLOTS, 0, e, k, it))
                    pe.transpose(x_bank[k % 2][:, 0:CAP], xg[:, k % GSLOTS, :], identf[0:CAP, 0:CAP]).then_inc(xT_ps, 1)
                if not isinstance(e, int) or 1 <= e <= E:
                    s = (k - 1) % UNROLL
                    pe.wait_ge(xT_ready, rnd * E + e)
                    pe.wait_ge(w_in[s // 2], 32 * ITERS * rnd + 32 * nth_use(UNROLL, 1, e, k, it))
                    for c in range(HC):
                        last = pe.matmul(h_bank[(k - 1) % 2][:, c * CAP:(c + 1) * CAP], w1_ring[:, s, c * P:(c + 1) * P],
                                         xT[:, (k - 1) % 2, :], start=True, stop=True)
                    last.then_inc(h_ps, 1)
                if not isinstance(e, int) or e >= 2:
                    s = (k - 2) % UNROLL
                    pe.wait_ge(hid_ready, 2 * (rnd * E + e - 1))
                    if not (first and isinstance(e, int) and e - 2 < 2):
                        pe.wait_ge(y_ready, rnd * E + e - 3)
                    for c in range(HC):
                        last = pe.matmul(y_bank[k % 2][0:CAP, 0:D], hidden[:, k % 2, c, :], w2_ring[:, s, c, :],
                                         start=(c == 0), stop=(c == HC - 1))
                    last.then_inc(y_ps, 1)

            expert_rounds(pe, step)
            pe.wait_ge(gmat_ready, 1)
            for c in range(NCH):
                if c:
                    pe.wait_ge(gT_ready, c)
                for t in chunk_tiles(c):
                    last = pe.transpose(rp_bank[0:E, t % TPC * P:(t % TPC + 1) * P], gmat[:, t, :], identf[:, :])
                last.then_inc(gT_ps, 1)
            for c in range(NCH):
                pe.wait_ge(gT_ready, c + 1)
                for t in chunk_tiles(c):
                    last = pe.matmul(banks[c][:, t % TPC * P:(t % TPC + 1) * P], gT[:, t * P:(t + 1) * P], b2_sb[:, :],
                                     start=True, stop=True)
                last.then_inc(bias_ps, 1)

        @block.vector
        def _(dve):
            steps = Steps(dve, dve_link)
            link = steps.link

            def tile(buf, t, n):
                return buf[0:n, t, :] if isinstance(t, int) else buf[:, bass.ds(t, 1), :].rearrange("p o d -> p (o d)")

            dve.memset(hx[:, NT - 1, :], 0.0).then_inc(dve_step, 1)
            dve.memset(mv[:, :, :], 1.0).then_inc(dve_step, 1)
            dve.memset(nmask[:, :, N:NP], -BIG).then_inc(dve_step, 1)
            dve.memset(parts[:, :, 0:3], 1.0).then_inc(dve_step, 1)
            dve.memset(parts[:, :, 3:6], 0.0).then_inc(dve_step, 1)
            dve.memset(parts[:, :, 15:18], 1.0).then_inc(dve_step, 1)
            dve.memset(hx[:, 0:NT - 1, D:D + 1], 1.0).then_inc(dve_step, 1)
            dve.wait_ge(dve_step, 7)
            dve.memset(hx[0:LAST, NT - 1, D:D + 1], 1.0).then_inc(dve_step, 1)
            dve.wait_ge(x_in, 16)
            dve.wait_ge(xl_in, 16)
            for t in range(NT):
                n = rows_of(t)
                last = dve.bn_stats(bn[0:n, t, :], x_sb[0:n, t, :])
            link(last)
            for t in range(NT):
                n = rows_of(t)
                last = dve.bn_aggr(mv[0:n, t, :], bn[0:n, t, :])
            last.then_inc(stats_ready, 1)
            dve.wait_ge(rstd_ready, 1)
            for t in range(NT):
                n = rows_of(t)
                last = dve.tensor_scalar(hx[0:n, t, 0:D], x_sb[0:n, t, :], mv[0:n, t, 0:1], rstd[0:n, t:t + 1],
                                         ALU.subtract, ALU.mult)
            last.then_inc(h_ready, 1)
            dve.wait_ge(small_in, 16 * LOADS)
            dve.wait_ge(pool_step, 5)
            dve.tensor_scalar(a2_bc[:, :], ones_f[:, :], a_sb[:, 1:2], None, ALU.mult).then_inc(a2_ready, 1)
            dve.wait_ge(w_ps, 1)
            link(dve.tensor_copy(w3[:, :, 0:2], rp_bank[:, 0:2 * NT].rearrange("p (t c) -> p t c", c=2)))
            link(dve.tensor_scalar(w3[:, :, 2], w3[:, :, 1], ALPHA, None, ALU.mult))
            dve.tensor_copy(w1_col[:, :], w3[:, :, 0])
            link(dve.tensor_scalar(aw1_col[:, :], w3[:, :, 0], ALPHA, None, ALU.mult))
            pq = parts[:, :, 6:15].rearrange("p t (g q) -> p t g q", q=3)
            link(dve.tensor_copy(pq[:, :, :, 0], w3[:, :, :]))
            link(dve.tensor_tensor(w3r[:, :, :], w3[:, :, :], pq[:, :, :, 0], ALU.subtract))
            link(dve.tensor_copy(pq[:, :, :, 1], w3r[:, :, :]))
            dve.tensor_tensor(pq[:, :, :, 2], w3r[:, :, :], pq[:, :, :, 1], ALU.subtract).then_inc(parts_ready, 1)
            dve.wait_ge(w2bc_ready, NCH)
            dve.wait_ge(const_made, CONST)

            def step(t, par):
                has_a, has_b, has_c1, has_c2 = stages(t)
                n = rows_of(t)
                q = (par + 1) % 2

                def add_relu(c):
                    k = len(chunk_tiles(c))
                    b = (par + c) % 2
                    dve.wait_ge(z_ps, 3 * t + c + 1)
                    dve.wait_ge(relu_ready, 3 * t + c + 1)
                    if not isinstance(t, int) or 3 * t + c >= 2:
                        dve.wait_ge(p_ready, 3 * t + c - 1)
                    dve.tensor_tensor(tiles3(z_sb[:, b, :], k, n), tiles3(relu_s[:, b, :], k, n),
                                      tiles3(z_bank[b], k, n), ALU.add).then_inc(z_ready, 1)

                if has_a:
                    m = rows_of(t + 1)
                    u = t + 1
                    dve.wait_ge(adj_in[q], loads16(u, q))
                    if not isinstance(t, int) or t >= 1:
                        dve.wait_ge(z_ps, 3 * t)
                    dve.tensor_scalar(nmask[0:m, q, 0:N], adj_sb[0:m, q, :], 0.0, -BIG, ALU.is_le,
                                      ALU.mult).then_inc(mask_ready, 1)
                if has_b:
                    add_relu(0)
                if has_c1:
                    m = rows_of(t - 1)
                    dve.wait_ge(o_ps, t)
                    if isinstance(t, int) and t == 1:
                        dve.wait_ge(hsum_ready, 2)
                    al = alone[0:m, t - 1:t] if isinstance(t, int) else alone[:, bass.ds(t - 1, 1)]
                    link(dve.scalar_tensor_tensor(o_sb[0:m, q, :], hsum[0:m, :], al, o_bank[q][0:m, 0:D + 1],
                                                  ALU.mult, ALU.add))
                    link(dve.reciprocal(rden[0:m, q:q + 1], o_sb[0:m, q, D:D + 1]))
                    link(dve.scalar_tensor_tensor(tile(x1, t - 1, m), o_sb[0:m, q, 0:D], rden[0:m, q:q + 1],
                                                  tile(x_sb, t - 1, m), ALU.mult, ALU.add))
                    link(dve.bn_stats(bn2[0:m, q, :], tile(x1, t - 1, m)))
                    dve.bn_aggr(mv2[0:m, q, :], bn2[0:m, q, :]).then_inc(mv2_ready, 1)
                if has_a:
                    m = rows_of(t + 1)
                    if not isinstance(t, int) or t >= 1:
                        dve.wait_ge(v_ready, t)
                    wait_apart(dve, mask_ready, t + 2)
                    link(dve.tensor_tensor_reduce(out=junk[0:m, q, :], in0=nmask[0:m, q, 0:N], in1=w2_bc[0:m, 0:N],
                                                  scale=1.0, scalar=-3e38, op0=ALU.add, op1=ALU.max,
                                                  accum_out=rmax[0:m, q:q + 1]))
                    al = alone[0:m, t + 1:t + 2] if isinstance(t, int) else alone[:, bass.ds(t + 1, 1)]
                    dve.tensor_scalar(al, rmax[0:m, q:q + 1], -BIG / 2, None, ALU.is_lt).then_inc(rowmax_ready, 1)
                if has_b:
                    add_relu(1)
                if has_c1:
                    m = rows_of(t - 1)
                    dve.wait_ge(mv2_ready, t)
                    if not isinstance(t, int) or t >= 3:
                        dve.wait_ge(xh2T_ps, t - 2)
                        dve.wait_ge(xh2_out[q], loads16(t - 3, q))
                    dve.wait_ge(rstd2_ready, t)
                    dve.tensor_scalar(xh2[0:m, q, :], tile(x1, t - 1, m), mv2[0:m, q, 0:1], rstd2[0:m, q:q + 1],
                                      ALU.subtract, ALU.mult).then_inc(xh2_ready, 1)
                if has_c2:
                    u = t - 2
                    m = rows_of(u)
                    dve.wait_ge(logit_ps, t - 1)
                    dve.tensor_tensor(logit[0:m, par, :], c_bank[0:m, 0:E], br_bc[0:m, :], ALU.add).then_inc(logit_ready, 1)
                    wait_apart(dve, logit_ready, t - 1)
                    link(dve.max(top8[0:m, par, :], logit[0:m, par, :]))
                    link(dve.max_index(idx8[0:m, par, :], top8[0:m, par, :], logit[0:m, par, :]))
                    ex = [exp2[0:m, k, u:u + 1] if isinstance(t, int) else exp2[:, k, bass.ds(u, 1)] for k in range(2)]
                    for k in range(2):
                        link(dve.tensor_copy(ex[k], idx8[0:m, par, k:k + 1]))
                    link(dve.tensor_copy(tile(top2, u, m), top8[0:m, par, 0:2]))
                    for k in range(2):
                        o = oh[0:m, k, u, :] if isinstance(t, int) else oh[:, k, bass.ds(u, 1), :].rearrange("p o e -> p (o e)")
                        ins = dve.tensor_scalar(o, iota_e[0:m, :], ex[k], None, ALU.is_equal)
                        if k == 0:
                            link(ins)
                        else:
                            ins.then_inc(oh_ready, 1)
                if has_b:
                    add_relu(2)

            attention_steps(dve, step, steps)

            dve.wait_ge(oh_ready, NT)
            dve.tensor_tensor(gden[:, :], top2[:, :, 1], top2[:, :, 0], ALU.subtract).then_inc(diff_ready, 1)
            link(dve.tensor_scalar(oh_lo[:, :, :, :], oh[:, :, :, :], tok_lo[:, 0:1], None, ALU.mult))
            for k in range(2):
                link(dve.tensor_tensor(oh_hi[:, k, :, :], oh[:, k, :, :], tile_base[:, :, :], ALU.mult))
            dve.wait_ge(rank_ps, 1)
            for bank, t0, t1 in ((banks[2], 0, 8), (banks[3], 8, NT)):
                link(dve.tensor_tensor(rowno[:, t0:t1, :], bank[:, 0:(t1 - t0) * E].rearrange("p (t e) -> p t e", e=E),
                                       row_of_e[:, t0:t1, :], ALU.add))
            link(dve.tensor_reduce(cnt[:, :], banks[3][:, 3 * E:4 * E], AX_X, ALU.max))
            for k in range(2):
                link(dve.tensor_tensor(picked[:, k, :, :], oh[:, k, :, :], rowno[:, :, :], ALU.mult))
            link(dve.tensor_reduce(ypos[:, :, :], picked[:, :, :, :], AX_X, ALU.add))
            dve.scalar_tensor_tensor(rank[:, :, :], exp2[:, :, :], -float(CAP), ypos[:, :, :], ALU.mult,
                                     ALU.add).then_inc(rank_ready, 1)
            dve.wait_ge(rank_ready, 1)

            def lists(rnd):
                for k in range(2):
                    dve.tensor_tensor(rank_oh[:, k, :, :], iota_r[:, :].unsqueeze(1).to_broadcast([P, NT, CAP]),
                                      rank[:, k, :].unsqueeze(2).to_broadcast([P, NT, CAP]), ALU.is_equal
                                      ).then_inc(rank_oh_ready, 1)
                dve.wait_ge(rank_oh_ready, 2 * rnd + 2)
                dve.tensor_scalar(rank[:, :, :], rank[:, :, :], -float(CAP), None, ALU.add).then_inc(rank_ready, 1)
                dve.wait_ge(tok_ps, rnd + 1)
                dve.tensor_copy(tok_i[:, :], c_bank[0:CAP, 0:E]).then_inc(tok_ready, 1)

            def hidden_of(rnd, e, k):
                dve.wait_ge(h_ps, rnd * E + e + 1)
                for c in range(HC):
                    dve.tensor_scalar(hidden[:, k % 2, c, :], h_bank[k % 2][:, c * CAP:(c + 1) * CAP],
                                      b1T[:, c, bass.ds(e, 1)], 0.0, ALU.add, ALU.max).then_inc(hid_ready, 1)

            lists(0)
            dve.tensor_copy(cnt_i[:, :], cnt[:, :]).then_inc(count_ready, 1)
            dve.tensor_copy(ypos_i[:, :, :], ypos[:, :, :]).then_inc(ypos_ready, 1)
            dve.wait_ge(gexp_ready, 1)
            link(dve.tensor_scalar(gden[:, :], ge[:, :], 1.0, None, ALU.add))
            link(dve.reciprocal(g1[:, :], gden[:, :]))
            link(dve.tensor_tensor(g2[:, :], ge[:, :], g1[:, :], ALU.mult))

            with dve.Fori(0, ITERS) as it:
                for k in range(UNROLL):
                    hidden_of(0, it * UNROLL + k, k)
            most = most_tokens(dve)
            with dve.If(most > CAP):
                with dve.Fori(1, ROUNDS) as rnd:
                    dve.wait_ge(rank_ready, rnd + 1)
                    dve.tensor_scalar(later[:, :, :], rank[:, :, :], 0.0, float((E - 1) * CAP), ALU.is_ge,
                                      ALU.mult).then_inc(later_ready, 1)
                    dve.wait_ge(later_ready, 2 * rnd - 1)
                    dve.tensor_tensor(ypos[:, :, :], ypos[:, :, :], later[:, :, :], ALU.add).then_inc(later_ready, 1)
                    dve.wait_ge(later_ready, 2 * rnd)
                    dve.wait_ge(tok_now_ready, rnd * (E // GSLOTS))
                    lists(rnd)
                    with dve.Fori(0, ITERS) as it:
                        for k in range(UNROLL):
                            hidden_of(rnd, it * UNROLL + k, k)
                dve.tensor_copy(ypos_i[:, :, :], ypos[:, :, :]).then_inc(ypos_ready, 1)
            for k, (g, dst) in enumerate(((g1, gmat2), (g2, gmat))):
                link(dve.tensor_tensor(dst[:, :, :], oh[:, k, :, :], g[:, :].unsqueeze(2).to_broadcast([P, NT, E]), ALU.mult))
            dve.tensor_tensor(gmat[:, :, :], gmat[:, :, :], gmat2[:, :, :], ALU.add).then_inc(gmat_ready, 1)
            for c in range(NCH):
                k = len(chunk_tiles(c))
                dve.wait_ge(bias_ps, c + 1)
                for t in chunk_tiles(c):
                    m = rows_of(t)
                    dve.tensor_tensor(x1[0:m, t, :], x1[0:m, t, :], banks[c][0:m, t % TPC * P:(t % TPC + 1) * P],
                                      ALU.add).then_inc(bias_done, 1)
            for t in range(NT):
                m = rows_of(t)
                dve.wait_ge(bias_done, t + 1)
                for k, g in enumerate((g1, g2)):
                    n = 2 * t + k
                    dve.wait_ge(yg_in[n % 8], 16 * (n // 8 + 1))
                    ins = dve.scalar_tensor_tensor(x1[0:m, t, :], yg[0:m, n % 8, :], g[0:m, t:t + 1], x1[0:m, t, :],
                                                   ALU.mult, ALU.add)
                    if k == 0:
                        link(ins)
                    else:
                        ins.then_inc(row_done, 1)


_INS = ['x', 'adj', 'L0_gnn_a', 'L0_ffn_Wr', 'L0_ffn_br', 'L0_ffn_W1', 'L0_ffn_b1', 'L0_ffn_W2', 'L0_ffn_b2']


def kernel(**inputs):
    import numpy as _np
    import concourse.bacc as _bacc
    from concourse import mybir as _mybir
    from concourse.bass_utils import run_bass_kernel_spmd as _run

    nc = _bacc.Bacc("TRN2", target_bir_lowering=False, num_devices=1)
    arrays, args = {}, []
    for name in _INS:
        v = _np.ascontiguousarray(inputs[name])
        arrays[f"in_{name}_dram"] = v
        args.append(nc.dram_tensor(f"in_{name}_dram", v.shape, _mybir.dt.from_np(v.dtype), kind="ExternalInput").ap())
    shape = tuple(inputs["x"].shape)
    args.append(nc.dram_tensor("out_0_dram", shape, _mybir.dt.float32, kind="ExternalOutput").ap())
    gat_moe(nc, *args)
    r = _run(nc, [arrays], core_ids=[0])
    return r.results[0]["out_0_dram"]
```

```python
from contextlib import ExitStack

import concourse.bass as bass
from concourse import mybir

F32 = mybir.dt.float32
BF16 = mybir.dt.bfloat16
I32 = mybir.dt.int32
U32 = mybir.dt.uint32
ALU = mybir.AluOpType
ACT = mybir.ActivationFunctionType
AX_X = mybir.AxisListType.X

P = 128
BANK = 512
BIG = 2.0 ** 53
ALPHA = 0.2
EPS = 1e-5
CAP = 96
UNROLL = 16
PAIRS = UNROLL // 2
GSLOTS = 8


class Steps:

    def __init__(self, eng, sem):
        self.eng, self.sem, self.n = eng, sem, 0

    def clear(self):
        self.eng.sem_clear(self.sem)
        self.n = 0

    def tick(self, ins):
        self.n += 1
        ins.then_inc(self.sem, 1)
        return self.n

    def after(self, n):
        self.eng.wait_ge(self.sem, n)

    def link(self, ins):
        self.after(self.tick(ins))


def gat_moe(nc, x, adj, a, Wr, br, W1, b1, W2, b2, out):
    N, D = x.shape
    E, _, H = W1.shape
    HC = H // P
    NT = -(-N // P)
    LAST = N - P * (NT - 1)
    NP = NT * P
    ROUNDS = -(-N // CAP)
    ITERS = E // UNROLL
    NCH = -(-NP // BANK)
    TPC = BANK // P
    assert D == P and H == 2 * P and NT % 2 == 1 and E % UNROLL == 0 and NCH == 3

    ctx = ExitStack()
    with ctx:
        def sb(name, shape, dt=F32):
            return ctx.enter_context(nc.sbuf_tensor(name, shape, dt))

        def sem(name):
            return ctx.enter_context(nc.semaphore(name))

        banks = [ctx.enter_context(nc.psum_tensor(f"bank{i}", [P, BANK], F32)) for i in range(8)]
        pt_bank, o_bank, xh2T_bank, c_bank = banks[0:3], banks[4:6], banks[6], banks[7]
        rp_bank = banks[6]
        x_bank, h_bank, y_bank = banks[0:2], banks[2:4], banks[4:6]

        xh2_dram = nc.dram_tensor("xh2_rows", [N, D], F32, kind="Internal").ap()
        y_dram = nc.dram_tensor("expert_rows", [ROUNDS * E * CAP, D], F32, kind="Internal").ap()

        x_sb = sb("x_sb", [P, NT, D])
        a_sb = sb("a_sb", [P, 2])
        Wr_sb = sb("Wr_sb", [P, E])
        br_bc = sb("br_bc", [P, E])
        b1_sb = sb("b1_sb", [E, H])
        b2_sb = sb("b2_sb", [E, D])
        identf = sb("identf", [P, P])
        identb = sb("identb", [P, P], BF16)
        before = sb("before", [P, P], BF16)
        ones_bf = sb("ones_bf", [P, P], BF16)
        ones_f = sb("ones_f", [P, P])
        iota_e = sb("iota_e", [P, E])
        iota_r = sb("iota_r", [P, CAP])
        row_of_e = sb("row_of_e", [P, NT, E])
        tok_lo = sb("tok_lo", [P, 1])
        tile_base = sb("tile_base", [P, NT, E], BF16)
        neg_half = sb("neg_half", [P, NT])
        bn = sb("bn", [P, NT, 6])
        mv = sb("mv", [P, NT, 2])
        ve = sb("ve", [P, NT])
        rstd = sb("rstd", [P, NT])
        hx = sb("hx", [P, NT, D + 1])
        hT = sb("hT", [P, NP])
        a2_bc = sb("a2_bc", [P, P])
        aw2_bc = sb("aw2_bc", [P, NP])
        w1s = sb("w1s", [P, NT])
        adj_sb = sb("adj_sb", [P, 2, N], I32)
        mask = sb("mask", [P, 2, N], BF16)
        low = sb("low", [P, 2, N])
        relu_s = sb("relu_s", [P, 2, N])
        soft = sb("soft", [P, 2, NP])
        zmin = sb("zmin", [P, 2])
        pT = sb("pT", [P, 2, NT, P])
        rden = sb("rden", [P, 2])
        x1 = sb("x1", [P, NT, D])
        bn2 = sb("bn2", [P, 2, 6])
        mv2 = sb("mv2", [P, 2, 2])
        ve2 = sb("ve2", [P, 2])
        rstd2 = sb("rstd2", [P, 2])
        xh2 = sb("xh2", [P, 2, D])
        xh2T = sb("xh2T", [P, 2, P])
        logit = sb("logit", [P, NT, E])
        top8 = sb("top8", [P, NT, 8])
        idx8 = sb("idx8", [P, NT, 8], U32)
        exp2 = sb("exp2", [P, 2, NT])
        oh = sb("oh", [P, 2, NT, E], BF16)
        ohcum = sb("ohcum", [P, NT + 1, E], BF16)
        ohsum = sb("ohsum", [P, NT, E], BF16)
        rowno = sb("rowno", [P, NT, E])
        picked = sb("picked", [P, 2, NT, E])
        ypos = sb("ypos", [P, 2, NT])
        ypos_i = sb("ypos_i", [P, 2, NT], I32)
        rank = sb("rank", [P, 2, NT])
        later = sb("later", [P, 2, NT])
        oh_lo = sb("oh_lo", [P, 2, NT, E], BF16)
        oh_hi = sb("oh_hi", [P, 2, NT, E], BF16)
        rank_oh = sb("rank_oh", [P, 2, NT, CAP], BF16)
        cnt = sb("cnt", [P, 1])
        cnt_i = sb("cnt_i", [P, 1], I32)
        tok_i = sb("tok_i", [CAP, E], I32)
        ge = sb("ge", [P, NT])
        gden = sb("gden", [P, NT])
        g1 = sb("g1", [P, NT])
        g2 = sb("g2", [P, NT])
        gmat = sb("gmat", [P, NT, E])
        gmat2 = sb("gmat2", [P, NT, E])
        gT = sb("gT", [E, NP])
        tok_now = sb("tok_now", [CAP, 2, GSLOTS], I32)
        xg = sb("xg", [CAP, GSLOTS, D])
        xT = sb("xT", [P, 2, CAP])
        w1_ring = sb("w1_ring", [P, UNROLL, H])
        w2_ring = sb("w2_ring", [P, UNROLL, HC, D])
        b1T = sb("b1T", [P, HC, E])
        hidden = sb("hidden", [P, 2, HC, CAP])
        y_sb = sb("y_sb", [CAP, 4, 2, D])
        yg = hT[:, 0:8 * D].rearrange("p (s d) -> p s d", s=8)

        x_in = [sem(f"x_in{i}") for i in range(NCH)]
        small_in = sem("small_in")
        adj_in = [sem(f"adj_in{i}") for i in range(2)]
        ident_ready = sem("ident_ready")
        filled = sem("filled")
        stats_ready = sem("stats_ready")
        rstd_ready = sem("rstd_ready")
        h_ready = sem("h_ready")
        hT_ps = sem("hT_ps")
        hT_ready = sem("hT_ready")
        w1_ps = sem("w1_ps")
        w1_ready = sem("w1_ready")
        w2bc_ps = sem("w2bc_ps")
        w2bc_ready = sem("w2bc_ready")
        a2_ready = sem("a2_ready")
        b1T_ps = sem("b1T_ps")
        b1T_ready = sem("b1T_ready")
        mask_ready = sem("mask_ready")
        low_ready = sem("low_ready")
        relu_ready = sem("relu_ready")
        z_ready = sem("z_ready")
        p_ready = sem("p_ready")
        pT_ps = sem("pT_ps")
        pT_act = sem("pT_act")
        pT_dve = sem("pT_dve")
        o_ps = sem("o_ps")
        xh2_ready = sem("xh2_ready")
        xh2T_ps = sem("xh2T_ps")
        xh2T_ready = sem("xh2T_ready")
        logit_ps = sem("logit_ps")
        logit_ready = sem("logit_ready")
        oh_ready = sem("oh_ready")
        ohcum_ready = sem("ohcum_ready")
        xh2_out = [sem(f"xh2_out{i}") for i in range(2)]
        zeros_ready = sem("zeros_ready")
        mv2_ready = sem("mv2_ready")
        rstd2_ready = sem("rstd2_ready")
        rank_ps = sem("rank_ps")
        diff_ready = sem("diff_ready")
        gexp_ready = sem("gexp_ready")
        rank_oh_ready = sem("rank_oh_ready")
        rank_ready = sem("rank_ready")
        later_ready = sem("later_ready")
        stores_landed = sem("stores_landed")
        tok_ps = sem("tok_ps")
        tok_ready = sem("tok_ready")
        count_ready = sem("count_ready")
        ypos_ready = sem("ypos_ready")
        gmat_ready = sem("gmat_ready")
        tok_now_ready = sem("tok_now_ready")
        xg_in = [sem(f"xg_in{i}") for i in range(GSLOTS)]
        w_in = [sem(f"w_in{i}") for i in range(PAIRS)]
        xT_ps = sem("xT_ps")
        xT_ready = sem("xT_ready")
        h_ps = sem("h_ps")
        hid_ready = sem("hid_ready")
        y_ps = sem("y_ps")
        y_ready = sem("y_ready")
        y_out = [sem(f"y_out{i}") for i in range(4)]
        gT_ps = sem("gT_ps")
        gT_ready = sem("gT_ready")
        bias_ps = sem("bias_ps")
        bias_done = sem("bias_done")
        yg_in = [sem(f"yg_in{i}") for i in range(8)]
        row_done = sem("row_done")
        out_written = sem("out_written")
        dve_link = sem("dve_link")
        pool_link = sem("pool_link")
        const_made = sem("const_made")
        passed = sem("passed")

        ZEROS = 5
        LOADS = 5
        STEADY0, STEADY1 = 3, 7
        rows_of = lambda t: P if isinstance(t, int) and t < NT - 1 or not isinstance(t, int) else LAST

        CHOICES = {8: slice(0, 3), 9: slice(3, 6), 10: slice(6, 9), 11: slice(9, 10), 12: slice(10, 11)}
        assert NT == 11
        CONST = 11

        def chunk_tiles(c):
            return list(range(c * TPC, min((c + 1) * TPC, NT)))

        def attention_steps(eng, step, steps=None):
            for t in range(-3, STEADY0):
                step(t, t % 2)
            with eng.Fori(STEADY0 // 2, STEADY1 // 2) as i:
                if steps:
                    steps.clear()
                step(i * 2 + 1, 1)
                step(i * 2 + 2, 0)
            if steps:
                steps.clear()
            for t in range(STEADY1, NT + 2):
                step(t, t % 2)

        def has(u):
            return not isinstance(u, int) or 0 <= u < NT

        def needs(eng, semaphore, value):
            if not isinstance(value, int) or value > 0:
                eng.wait_ge(semaphore, value)

        def wait_apart(eng, semaphore, value):
            eng.wait_ge(semaphore, value)
            if not isinstance(value, int):
                eng.sem_inc(passed, 1)

        def tiles3(buf, k, n):
            return buf[:, 0:k * P].rearrange("p (t c) -> p t c", c=P)[:, :, 0:n]

        def loads16(u, q):
            return (u - q) * 8 + 16

        def expert_rounds(eng, step):
            def one(rnd, first):
                for e in range(UNROLL):
                    step(rnd, e, e, None, first)
                with eng.Fori(1, ITERS) as it:
                    for k in range(UNROLL):
                        step(rnd, it * UNROLL + k, k, it, first)
                for e in (E, E + 1):
                    step(rnd, e, e - E, None, first)
            one(0, True)
            most = most_tokens(eng)
            with eng.If(most > CAP):
                with eng.Fori(1, ROUNDS) as rnd:
                    one(rnd, False)

        def most_tokens(eng):
            eng.wait_ge(count_ready, 1)
            return eng.value_load(cnt_i[0:1, 0:1], min_val=0, max_val=N)

        def nth_use(slots, back, e, k, it):
            if isinstance(e, int):
                return (e - back) // slots + 1
            return it * (UNROLL // slots) + (k - back) // slots + 1

        block = ctx.enter_context(nc.Block())

        @block.sync
        def _(sp):
            for c in range(NCH):
                ts = [t for t in chunk_tiles(c) if rows_of(t) == P]
                sp.dma_start(x_sb[:, ts[0]:ts[-1] + 1, :],
                             x[P * ts[0]:P * (ts[-1] + 1), :].rearrange("(t p) d -> p t d", p=P)).then_inc(x_in[c], 16)
                if c == NCH - 1:
                    sp.dma_start(x_sb[0:LAST, NT - 1, :], x[P * (NT - 1):N, :]).then_inc(x_in[c], 16)
            sp.dma_start(adj_sb[:, 0, :], adj[0:P, :]).then_inc(adj_in[0], 16)
            sp.dma_start(adj_sb[:, 1, :], adj[P:2 * P, :]).then_inc(adj_in[1], 16)

            def load_weights(it, pair, e0):
                sp.dma_start(w1_ring[:, 2 * pair:2 * pair + 2, :],
                             W1[bass.ds(e0, 2), :, :].rearrange("e p h -> p e h")).then_inc(w_in[pair], 16)
                sp.dma_start(w2_ring[:, 2 * pair:2 * pair + 2, :, :].rearrange("p e c d -> p (e c) d"),
                             W2[bass.ds(e0, 2), :, :].rearrange("e (c p) d -> p (e c) d", p=P)).then_inc(w_in[pair], 16)

            def step(t, par):
                q = (par + 1) % 2
                if has(t + 3) and not (isinstance(t, int) and t + 3 < 2):
                    n = rows_of(t + 3)
                    sp.wait_ge(mask_ready, t + 2)
                    sp.dma_start(adj_sb[0:n, q, :], adj[bass.ds((t + 3) * P, n), :]).then_inc(adj_in[q], 16)
                if isinstance(t, int) and -1 <= t < 3:
                    for k in (2 * t + 2, 2 * t + 3):
                        load_weights(0, k, 2 * k)
                if has(t - 2):
                    sp.wait_ge(xh2_ready, t - 1)
                    n = rows_of(t - 2)
                    sp.dma_start(xh2_dram[bass.ds((t - 2) * P, n), :], xh2[0:n, par, :]).then_inc(xh2_out[par], 16)

            attention_steps(sp, step)

            def weights_round(rnd):
                with sp.Fori(0, ITERS - 1) as it:
                    for k in range(PAIRS):
                        sp.wait_ge(y_ps, rnd * E + it * UNROLL + 2 * k + 2)
                        load_weights(None, k, (it + 1) * UNROLL + 2 * k)

            weights_round(0)
            most = most_tokens(sp)
            with sp.If(most > CAP):
                with sp.Fori(1, ROUNDS) as rnd:
                    for k in range(PAIRS):
                        sp.wait_ge(y_ps, rnd * E - UNROLL + 2 * k + 2)
                        load_weights(None, k, 2 * k)
                    weights_round(rnd)
            for t in range(NT):
                sp.wait_ge(row_done, t + 1)
                n = rows_of(t)
                sp.dma_start(out[t * P:t * P + n, :], x1[0:n, t, :]).then_inc(out_written, 16)
            sp.wait_ge(out_written, 16 * NT)

        @block.gpsimd
        def _(pool):
            steps = Steps(pool, pool_link)
            link = steps.link
            pool.memset(identf[:, :], 0.0).then_inc(filled, 1)
            pool.memset(ones_f[:, :], 1.0).then_inc(filled, 1)
            pool.memset(neg_half[:, :], -0.5).then_inc(filled, 1)
            pool.wait_ge(filled, 3)
            pool.affine_select(out=identf[:, :], in_=identf[:, :], compare_op=ALU.not_equal, fill=1.0, base=0,
                               pattern=[[-1, P]], channel_multiplier=1).then_inc(ident_ready, 1)
            for c in range(NCH):
                ts = slice(c * TPC, min((c + 1) * TPC, NT))
                pool.wait_ge(stats_ready, c + 1)
                link(pool.tensor_scalar(ve[:, ts], mv[:, ts, 1], EPS, None, ALU.add))
                pool.tensor_tensor(rstd[:, ts], ve[:, ts], neg_half[:, ts], ALU.pow).then_inc(rstd_ready, 1)
            pool.wait_ge(w2bc_ready, NCH)

            def constants():
                pool.memset(ones_bf[:, :], 1.0).then_inc(const_made, 1)
                pool.memset(oh[:, :, NT - 1, :], 0.0).then_inc(const_made, 1)
                pool.memset(exp2[:, :, NT - 1], 0.0).then_inc(const_made, 1)
                pool.memset(top8[:, NT - 1, :], 0.0).then_inc(const_made, 1)
                pool.memset(ohcum[:, 0, :], 0.0).then_inc(const_made, 1)
                pool.iota(iota_e[:, :], [[1, E]], base=0, channel_multiplier=0,
                          allow_small_or_imprecise_dtypes=True).then_inc(const_made, 1)
                pool.wait_ge(const_made, 6)

            def more_constants():
                pool.affine_select(out=before[:, :], in_=ones_bf[:, :], compare_op=ALU.is_gt, fill=0.0, base=0,
                                   pattern=[[1, P]], channel_multiplier=-1).then_inc(const_made, 1)
                pool.iota(iota_r[:, :], [[1, CAP]], base=0, channel_multiplier=0,
                          allow_small_or_imprecise_dtypes=True).then_inc(const_made, 1)
                pool.iota(row_of_e[:, :, :], [[0, NT], [CAP, E]], base=0, channel_multiplier=0,
                          allow_small_or_imprecise_dtypes=True).then_inc(const_made, 1)
                pool.iota(tok_lo[:, :], [[0, 1]], base=0, channel_multiplier=1,
                          allow_small_or_imprecise_dtypes=True).then_inc(const_made, 1)
                pool.iota(tile_base[:, :, :], [[P, NT], [0, E]], base=0, channel_multiplier=0,
                          allow_small_or_imprecise_dtypes=True).then_inc(const_made, 1)

            def step(t, par):
                q = (par + 1) % 2
                if has(t + 2):
                    n = rows_of(t + 2)
                    wait_apart(pool, mask_ready, t + 3)
                    needs(pool, z_ready, t + 1)
                    if not isinstance(t, int):
                        pool.sem_inc(passed, 1)
                    pool.tensor_tensor(low[0:n, par, :], mask[0:n, par, :], aw2_bc[0:n, 0:N], ALU.add).then_inc(low_ready, 1)
                if has(t - 1):
                    n = rows_of(t - 1)
                    wait_apart(pool, mv2_ready, t)
                    link(pool.tensor_scalar(ve2[0:n, q:q + 1], mv2[0:n, q, 1:2], EPS, None, ALU.add))
                    pool.tensor_tensor(rstd2[0:n, q:q + 1], ve2[0:n, q:q + 1], neg_half[0:n, 0:1],
                                       ALU.pow).then_inc(rstd2_ready, 1)
                if isinstance(t, int):
                    if t == STEADY1:
                        constants()
                    if t == NT - 2:
                        more_constants()
                    if t in CHOICES:
                        ts = CHOICES[t]
                        pool.wait_ge(oh_ready, ts.stop)
                        link(pool.tensor_tensor(ohsum[:, ts, :], oh[:, 0, ts, :], oh[:, 1, ts, :], ALU.add))
                        for u in range(ts.start, ts.stop):
                            if u:
                                pool.wait_ge(ohcum_ready, u)
                            pool.tensor_tensor(ohcum[:, u + 1, :], ohcum[:, u, :], ohsum[:, u, :],
                                               ALU.add).then_inc(ohcum_ready, 1)

            attention_steps(pool, step, steps)

            for par, k in ((0, (NT + 1) // 2), (1, NT // 2)):
                pool.wait_ge(xh2_out[par], 16 * k)

            def gathers(rnd):
                wait_apart(pool, tok_ready, rnd + 1)
                with pool.Fori(0, ITERS) as it:
                    for k in range(UNROLL):
                        half, s = k // GSLOTS, k % GSLOTS
                        if s == 0:
                            pool.tensor_copy(tok_now[:, half, :],
                                             tok_i[:, bass.ds(it * UNROLL + half * GSLOTS, GSLOTS)]).then_inc(tok_now_ready, 1)
                            pool.wait_ge(tok_now_ready, rnd * (E // GSLOTS) + it * 2 + half + 1)
                        wait_apart(pool, xT_ps, rnd * E + it * UNROLL + k + 1)
                        pool.indirect_dma_start(xg[:, s, :], None, xh2_dram,
                                                bass.IndirectOffsetOnAxis(ap=tok_now[:, half, s:s + 1], axis=0)
                                                ).then_inc(xg_in[s], 16)
                for k in range(4):
                    pool.wait_ge(y_out[k], 16 * (E // 8) * (rnd + 1))

            def combine(table, ready):
                pool.wait_ge(ypos_ready, ready)
                for t in range(NT):
                    for k in range(2):
                        n = 2 * t + k
                        if n >= 8:
                            pool.wait_ge(row_done, (n - 8) // 2 + 1)
                        pool.indirect_dma_start(yg[:, n % 8, :], None, table,
                                                bass.IndirectOffsetOnAxis(ap=ypos_i[:, k, t:t + 1], axis=0)
                                                ).then_inc(yg_in[n % 8], 16)

            gathers(0)
            most = most_tokens(pool)
            with pool.If(most > CAP):
                with pool.Fori(1, ROUNDS) as rnd:
                    gathers(rnd)
                combine(y_dram, 2)
            with pool.Else():
                combine(y_dram[0:E * CAP, :], 1)

        @block.scalar
        def _(act):
            act.dma_start(a_sb[:, :], a.rearrange("(c p) o -> p (c o)", p=P),
                          allow_slow_non_contiguous=True).then_inc(small_in, 16)
            act.dma_start(Wr_sb[:, :], Wr).then_inc(small_in, 16)
            act.dma_start(br_bc[:, :], br.unsqueeze(0).to_broadcast([P, E])).then_inc(small_in, 16)
            act.dma_start(b1_sb[:, :], b1).then_inc(small_in, 16)
            act.dma_start(b2_sb[:, :], b2).then_inc(small_in, 16)
            for c in range(NCH):
                w = min(BANK, NP - c * BANK)
                act.wait_ge(hT_ps, c + 1)
                act.copy(hT[:, c * BANK:c * BANK + w], banks[c][:, 0:w]).then_inc(hT_ready, 1)
            for c in range(NCH):
                w = min(BANK, NP - c * BANK)
                act.wait_ge(w2bc_ps, c + 1)
                act.copy(aw2_bc[:, c * BANK:c * BANK + w], banks[3 + c][:, 0:w]).then_inc(w2bc_ready, 1)
            act.wait_ge(w1_ready, 1)
            act.wait_ge(w2bc_ready, NCH)

            def step(t, par):
                n = rows_of(t)
                q = (par + 1) % 2

                def transposed(c):
                    k = len(chunk_tiles(c))
                    act.wait_ge(pT_ps, 3 * t + c + 1)
                    needs(act, o_ps, t - 1)
                    act.copy(pT[:, par, c * TPC:c * TPC + k, 0:n], tiles3(pt_bank[c], k, n)).then_inc(pT_act, 1)

                if has(t):
                    transposed(0)
                if has(t + 2):
                    m = rows_of(t + 2)
                    needs(act, z_ready, t + 1)
                    w1 = w1s[0:m, t + 2:t + 3] if isinstance(t, int) else w1s[:, bass.ds(t + 2, 1)]
                    act.activation(relu_s[0:m, par, :], aw2_bc[0:m, 0:N], ACT.Relu, bias=w1,
                                   scale=(1.0 - ALPHA) / ALPHA).then_inc(relu_ready, 1)
                if has(t):
                    transposed(2)
                if has(t - 2):
                    m = rows_of(t - 2)
                    act.wait_ge(xh2T_ps, t - 1)
                    act.copy(xh2T[:, par, 0:m], xh2T_bank[:, 0:m]).then_inc(xh2T_ready, 1)
                if has(t + 1):
                    m = rows_of(t + 1)
                    act.wait_ge(z_ready, t + 2)
                    act.activation(soft[0:m, q, 0:N], soft[0:m, q, 0:N], ACT.Exp, bias=zmin[0:m, q:q + 1],
                                   scale=-1.0).then_inc(p_ready, 1)
                if isinstance(t, int) and t == -1:
                    act.wait_ge(b1T_ps, 1)
                    act.copy(b1T[:, :, :], c_bank[:, 0:HC * E].rearrange("p (c e) -> p c e", c=HC)).then_inc(b1T_ready, 1)

            attention_steps(act, step)
            act.wait_ge(diff_ready, 1)
            act.activation(ge[:, :], gden[:, :], ACT.Exp).then_inc(gexp_ready, 1)

            def step(rnd, e, k, it, first):
                if not isinstance(e, int) or e < E:
                    act.wait_ge(xT_ps, GSLOTS + rnd * E + e + 1)
                    act.copy(xT[:, k % 2, :], x_bank[k % 2][:, 0:CAP]).then_inc(xT_ready, 1)
                if not isinstance(e, int) or e >= 2:
                    q = (k - 2) % UNROLL // 2
                    u = (k - 2) % 2
                    if u == 0 and not (first and isinstance(e, int) and e - 2 < 8):
                        act.wait_ge(y_out[q % 4], 16 * (E // 8) * rnd + 16 * (nth_use(8, 2, e, k, it) - 1))
                    act.wait_ge(y_ps, rnd * E + e - 1)
                    act.copy(y_sb[:, q % 4, u, :], y_bank[k % 2][0:CAP, 0:D]).then_inc(y_ready, 1)
                    if u == 1:
                        act.wait_ge(y_ready, rnd * E + e - 1)
                        rows = y_dram.rearrange("(e r) d -> r e d", r=CAP)
                        act.dma_start(rows[:, bass.ds(rnd * E + e - 3, 2), :],
                                      y_sb[:, q % 4, :, :]).then_inc(y_out[q % 4], 16)

            expert_rounds(act, step)
            for c in range(NCH):
                w = min(BANK, NP - c * BANK)
                act.wait_ge(gT_ps, c + 1)
                act.copy(gT[:, c * BANK:c * BANK + w], rp_bank[0:E, 0:w]).then_inc(gT_ready, 1)

        @block.tensor
        def _(pe):
            pe.sem_inc(xT_ps, GSLOTS)
            pe.wait_ge(ident_ready, 1)

            def h_transposed(c):
                pe.wait_ge(h_ready, c + 1)
                for t in chunk_tiles(c):
                    last = pe.transpose(banks[c][:, t % TPC * P:(t % TPC + 1) * P], hx[:, t, 0:D], identf[:, :])
                last.then_inc(hT_ps, 1)

            def w2_broadcast(c):
                w = min(BANK, NP - c * BANK)
                pe.wait_ge(hT_ready, c + 1)
                pe.matmul(banks[3 + c][:, 0:w], a2_bc[:, :], hT[:, c * BANK:c * BANK + w],
                          start=True, stop=True).then_inc(w2bc_ps, 1)

            h_transposed(0)
            h_transposed(1)
            pe.wait_ge(a2_ready, 1)
            w2_broadcast(0)
            h_transposed(2)
            w2_broadcast(1)
            w2_broadcast(2)
            for t in range(NT):
                last = pe.matmul(rp_bank[:, t:t + 1], hT[:, t * P:(t + 1) * P], a_sb[:, 0:1], start=True, stop=True)
            last.then_inc(w1_ps, 1)
            for c in range(HC):
                last = pe.transpose(c_bank[:, c * E:(c + 1) * E], b1_sb[:, c * P:(c + 1) * P], identf[0:E, 0:E])
            last.then_inc(b1T_ps, 1)
            pe.wait_ge(w1_ready, 1)
            pe.wait_ge(b1T_ready, 1)
            pe.wait_ge(zeros_ready, ZEROS)

            def step(t, par):
                n = rows_of(t)

                def transpose_p(c):
                    if c == 0:
                        pe.wait_ge(p_ready, t + 1)
                    needs(pe, pT_dve if c == 1 else pT_act, (2 * t - 1, t, 2 * t)[c])
                    for j in chunk_tiles(c):
                        o = j % TPC * P
                        last = pe.transpose(pt_bank[c][:, o:o + n], soft[0:n, par, j * P:(j + 1) * P], identf[0:n, 0:n])
                    last.then_inc(pT_ps, 1)

                def weigh(c):
                    pe.wait_ge(pT_dve if c == 1 else pT_act, (2 * t + 1, t + 1, 2 * t + 2)[c])
                    if c == 0:
                        needs(pe, mv2_ready, t - 1)
                    for j in chunk_tiles(c):
                        last = pe.matmul(o_bank[par][0:n, 0:D + 1], pT[:, par, j, 0:n], hx[:, j, :],
                                         start=(j == 0), stop=(j == NT - 1))
                    if c == NCH - 1:
                        last.then_inc(o_ps, 1)

                if has(t):
                    transpose_p(0)
                    transpose_p(1)
                if has(t - 2):
                    m = rows_of(t - 2)
                    pe.wait_ge(xh2_ready, t - 1)
                    needs(pe, xh2T_ready, t - 2)
                    pe.transpose(xh2T_bank[:, 0:m], xh2[0:m, par, :], identf[0:m, 0:m]).then_inc(xh2T_ps, 1)
                if has(t):
                    transpose_p(2)
                    weigh(0)
                    weigh(1)
                if has(t - 2):
                    pe.wait_ge(xh2T_ready, t - 1)
                    needs(pe, logit_ready, t - 2)
                    pe.matmul(c_bank[0:m, 0:E], xh2T[:, par, 0:m], Wr_sb[:, :], start=True, stop=True).then_inc(logit_ps, 1)
                if has(t):
                    weigh(2)

            attention_steps(pe, step)

            pe.wait_ge(ohcum_ready, NT)
            pe.wait_ge(const_made, CONST)
            for bank, t0, t1 in ((banks[2], 0, 8), (banks[3], 8, NT)):
                w = (t1 - t0) * E
                pe.matmul(bank[:, 0:w], before[:, :], oh[:, 0, t0:t1, :], start=True, stop=False)
                pe.matmul(bank[:, 0:w], before[:, :], oh[:, 1, t0:t1, :], start=False, stop=False)
                pe.matmul(bank[:, 0:w], ones_bf[:, :], ohcum[:, t0:t1, :], start=False, stop=True)
            pe.matmul(banks[3][:, 3 * E:4 * E], ones_bf[:, :], ohcum[:, NT, :], start=True, stop=True).then_inc(rank_ps, 1)

            def lists(rnd):
                for k in range(2):
                    pe.wait_ge(rank_oh_ready, 2 * rnd + k + 1)
                    for t in range(NT):
                        for v, buf in enumerate((oh_lo, oh_hi)):
                            last = pe.matmul(c_bank[0:CAP, 0:E], rank_oh[:, k, t, :], buf[:, k, t, :],
                                             start=(k == 0 and t == 0 and v == 0), stop=(k == 1 and t == NT - 1 and v == 1))
                last.then_inc(tok_ps, 1)

            def step(rnd, e, k, it, first):
                if isinstance(e, int) and e == 0:
                    lists(rnd)
                if not isinstance(e, int) or e < E:
                    pe.wait_ge(xg_in[k % GSLOTS], 16 * (E // GSLOTS) * rnd + 16 * nth_use(GSLOTS, 0, e, k, it))
                    pe.transpose(x_bank[k % 2][:, 0:CAP], xg[:, k % GSLOTS, :], identf[0:CAP, 0:CAP]).then_inc(xT_ps, 1)
                if not isinstance(e, int) or 1 <= e <= E:
                    s = (k - 1) % UNROLL
                    pe.wait_ge(xT_ready, rnd * E + e)
                    pe.wait_ge(w_in[s // 2], 32 * ITERS * rnd + 32 * nth_use(UNROLL, 1, e, k, it))
                    for c in range(HC):
                        last = pe.matmul(h_bank[(k - 1) % 2][:, c * CAP:(c + 1) * CAP], w1_ring[:, s, c * P:(c + 1) * P],
                                         xT[:, (k - 1) % 2, :], start=True, stop=True)
                    last.then_inc(h_ps, 1)
                if not isinstance(e, int) or e >= 2:
                    s = (k - 2) % UNROLL
                    pe.wait_ge(hid_ready, 2 * (rnd * E + e - 1))
                    if not (first and isinstance(e, int) and e - 2 < 2):
                        pe.wait_ge(y_ready, rnd * E + e - 3)
                    for c in range(HC):
                        last = pe.matmul(y_bank[k % 2][0:CAP, 0:D], hidden[:, k % 2, c, :], w2_ring[:, s, c, :],
                                         start=(c == 0), stop=(c == HC - 1))
                    last.then_inc(y_ps, 1)

            expert_rounds(pe, step)
            pe.wait_ge(gmat_ready, 1)
            for c in range(NCH):
                if c:
                    pe.wait_ge(gT_ready, c)
                for t in chunk_tiles(c):
                    last = pe.transpose(rp_bank[0:E, t % TPC * P:(t % TPC + 1) * P], gmat[:, t, :], identf[:, :])
                last.then_inc(gT_ps, 1)
            for c in range(NCH):
                pe.wait_ge(gT_ready, c + 1)
                for t in chunk_tiles(c):
                    last = pe.matmul(banks[c][:, t % TPC * P:(t % TPC + 1) * P], gT[:, t * P:(t + 1) * P], b2_sb[:, :],
                                     start=True, stop=True)
                last.then_inc(bias_ps, 1)

        @block.vector
        def _(dve):
            steps = Steps(dve, dve_link)
            link = steps.link

            def tile(buf, t, n):
                return buf[0:n, t, :] if isinstance(t, int) else buf[:, bass.ds(t, 1), :].rearrange("p o d -> p (o d)")

            dve.memset(mv[:, :, :], 1.0).then_inc(zeros_ready, 1)
            dve.memset(hx[:, NT - 1, :], 0.0).then_inc(zeros_ready, 1)
            dve.memset(hx[:, 0:NT - 1, D:D + 1], 1.0).then_inc(zeros_ready, 1)
            dve.memset(soft[:, :, N:NP], 0.0).then_inc(zeros_ready, 1)
            dve.wait_ge(zeros_ready, 4)
            dve.memset(hx[0:LAST, NT - 1, D:D + 1], 1.0).then_inc(zeros_ready, 1)

            def statistics(c):
                dve.wait_ge(x_in[c], 16 if c < NCH - 1 else 32)
                for t in chunk_tiles(c):
                    n = rows_of(t)
                    last = dve.bn_stats(bn[0:n, t, :], x_sb[0:n, t, :])
                link(last)
                for t in chunk_tiles(c):
                    n = rows_of(t)
                    last = dve.bn_aggr(mv[0:n, t, :], bn[0:n, t, :])
                last.then_inc(stats_ready, 1)

            def normalise(c):
                dve.wait_ge(rstd_ready, c + 1)
                for t in chunk_tiles(c):
                    n = rows_of(t)
                    last = dve.tensor_scalar(hx[0:n, t, 0:D], x_sb[0:n, t, :], mv[0:n, t, 0:1], rstd[0:n, t:t + 1],
                                             ALU.subtract, ALU.mult)
                last.then_inc(h_ready, 1)

            statistics(0)
            statistics(1)
            normalise(0)
            statistics(2)
            normalise(1)
            normalise(2)
            dve.wait_ge(small_in, 16 * LOADS)
            dve.wait_ge(filled, 3)
            dve.tensor_scalar(a2_bc[:, :], ones_f[:, :], a_sb[:, 1:2], ALPHA, ALU.mult, ALU.mult).then_inc(a2_ready, 1)

            def choose(ts):
                dve.wait_ge(const_made, 6)
                dve.wait_ge(logit_ready, ts.stop)
                for u in range(ts.start, ts.stop):
                    m = rows_of(u)
                    n = steps.tick(dve.max(top8[0:m, u, :], logit[0:m, u, :]))
                for u in range(ts.start, ts.stop):
                    m = rows_of(u)
                    steps.after(n - (ts.stop - 1 - u))
                    last = dve.max_index(idx8[0:m, u, :], top8[0:m, u, :], logit[0:m, u, :])
                link(last)
                m = rows_of(ts.stop - 1)
                link(dve.tensor_copy(exp2[0:m, :, ts], idx8[0:m, ts, 0:2].rearrange("p t k -> p k t")))
                g = ts.stop - ts.start
                for k in range(2):
                    ins = dve.tensor_tensor(oh[0:m, k, ts, :], iota_e[0:m, :].unsqueeze(1).to_broadcast([m, g, E]),
                                            exp2[0:m, k, ts].unsqueeze(2).to_broadcast([m, g, E]), ALU.is_equal)
                    if k == 0:
                        link(ins)
                    else:
                        ins.then_inc(oh_ready, g)

            def step(t, par):
                n = rows_of(t)
                q = (par + 1) % 2
                if has(t + 1):
                    m = rows_of(t + 1)
                    dve.wait_ge(low_ready, t + 2)
                    dve.wait_ge(relu_ready, t + 2)
                    needs(dve, pT_ps, 3 * t)
                    if not isinstance(t, int):
                        dve.sem_inc(passed, 1)
                    dve.tensor_tensor_reduce(out=soft[0:m, q, 0:N], in0=relu_s[0:m, q, :], in1=low[0:m, q, :],
                                             scale=-1.0, scalar=3e38, op0=ALU.add, op1=ALU.min,
                                             accum_out=zmin[0:m, q:q + 1]).then_inc(z_ready, 1)
                if has(t - 1):
                    u = rows_of(t - 1)
                    dve.wait_ge(o_ps, t)
                    divided = steps.tick(dve.reciprocal(rden[0:u, q:q + 1], o_bank[q][0:u, D:D + 1]))
                if has(t):
                    k = len(chunk_tiles(1))
                    dve.wait_ge(pT_ps, 3 * t + 2)
                    needs(dve, o_ps, t - 1)
                    dve.tensor_copy(pT[:, par, TPC:TPC + k, 0:n], tiles3(pt_bank[1], k, n)).then_inc(pT_dve, 1)
                if has(t - 1):
                    steps.after(divided)
                    summed = steps.tick(dve.scalar_tensor_tensor(tile(x1, t - 1, u), o_bank[q][0:u, 0:D], rden[0:u, q:q + 1],
                                                                 tile(x_sb, t - 1, u), ALU.mult, ALU.add))
                if has(t + 3):
                    m = rows_of(t + 3)
                    dve.wait_ge(adj_in[q], loads16(t + 3, q))
                    needs(dve, low_ready, t + 2)
                    dve.tensor_scalar(mask[0:m, q, :], adj_sb[0:m, q, :], 0.0, -BIG, ALU.is_le,
                                      ALU.mult).then_inc(mask_ready, 1)
                if has(t - 1):
                    steps.after(summed)
                    link(dve.bn_stats(bn2[0:u, q, :], tile(x1, t - 1, u)))
                    dve.bn_aggr(mv2[0:u, q, :], bn2[0:u, q, :]).then_inc(mv2_ready, 1)
                if has(t - 2):
                    m = rows_of(t - 2)
                    dve.wait_ge(logit_ps, t - 1)
                    dve.tensor_tensor(tile(logit, t - 2, m), c_bank[0:m, 0:E], br_bc[0:m, :], ALU.add).then_inc(logit_ready, 1)
                if has(t - 1):
                    if not isinstance(t, int) or t >= 3:
                        dve.wait_ge(xh2T_ps, t - 2)
                        dve.wait_ge(xh2_out[q], loads16(t - 3, q))
                    dve.wait_ge(rstd2_ready, t)
                    dve.tensor_scalar(xh2[0:u, q, :], tile(x1, t - 1, u), mv2[0:u, q, 0:1], rstd2[0:u, q:q + 1],
                                      ALU.subtract, ALU.mult).then_inc(xh2_ready, 1)
                if isinstance(t, int) and t == -2:
                    dve.wait_ge(w1_ps, 1)
                    dve.tensor_scalar(w1s[:, :], rp_bank[:, 0:NT], 1.0 - ALPHA, None, ALU.mult).then_inc(w1_ready, 1)
                if isinstance(t, int) and t in CHOICES:
                    choose(CHOICES[t])

            attention_steps(dve, step, steps)

            dve.wait_ge(oh_ready, NT)
            dve.wait_ge(const_made, CONST)
            dve.tensor_tensor(gden[:, :], top8[:, :, 1], top8[:, :, 0], ALU.subtract).then_inc(diff_ready, 1)
            link(dve.tensor_scalar(oh_lo[:, :, :, :], oh[:, :, :, :], tok_lo[:, 0:1], None, ALU.mult))
            for k in range(2):
                link(dve.tensor_tensor(oh_hi[:, k, :, :], oh[:, k, :, :], tile_base[:, :, :], ALU.mult))
            dve.wait_ge(rank_ps, 1)
            for bank, t0, t1 in ((banks[2], 0, 8), (banks[3], 8, NT)):
                link(dve.tensor_tensor(rowno[:, t0:t1, :], bank[:, 0:(t1 - t0) * E].rearrange("p (t e) -> p t e", e=E),
                                       row_of_e[:, t0:t1, :], ALU.add))
            link(dve.tensor_reduce(cnt[:, :], banks[3][:, 3 * E:4 * E], AX_X, ALU.max))
            for k in range(2):
                link(dve.tensor_tensor(picked[:, k, :, :], oh[:, k, :, :], rowno[:, :, :], ALU.mult))
            link(dve.tensor_reduce(ypos[:, :, :], picked[:, :, :, :], AX_X, ALU.add))
            dve.scalar_tensor_tensor(rank[:, :, :], exp2[:, :, :], -float(CAP), ypos[:, :, :], ALU.mult,
                                     ALU.add).then_inc(rank_ready, 1)
            dve.wait_ge(rank_ready, 1)

            def lists(rnd):
                for k in range(2):
                    dve.tensor_tensor(rank_oh[:, k, :, :], iota_r[:, :].unsqueeze(1).to_broadcast([P, NT, CAP]),
                                      rank[:, k, :].unsqueeze(2).to_broadcast([P, NT, CAP]), ALU.is_equal
                                      ).then_inc(rank_oh_ready, 1)
                dve.wait_ge(rank_oh_ready, 2 * rnd + 2)
                dve.tensor_scalar(rank[:, :, :], rank[:, :, :], -float(CAP), None, ALU.add).then_inc(rank_ready, 1)
                dve.wait_ge(tok_ps, rnd + 1)
                dve.tensor_copy(tok_i[:, :], c_bank[0:CAP, 0:E]).then_inc(tok_ready, 1)

            def hidden_of(rnd, e, k):
                dve.wait_ge(h_ps, rnd * E + e + 1)
                for c in range(HC):
                    dve.tensor_scalar(hidden[:, k % 2, c, :], h_bank[k % 2][:, c * CAP:(c + 1) * CAP],
                                      b1T[:, c, bass.ds(e, 1)], 0.0, ALU.add, ALU.max).then_inc(hid_ready, 1)

            lists(0)
            dve.wait_ge(b1T_ready, 1)
            dve.tensor_copy(cnt_i[:, :], cnt[:, :]).then_inc(count_ready, 1)
            dve.tensor_copy(ypos_i[:, :, :], ypos[:, :, :]).then_inc(ypos_ready, 1)
            dve.wait_ge(gexp_ready, 1)
            link(dve.tensor_scalar(gden[:, :], ge[:, :], 1.0, None, ALU.add))
            link(dve.reciprocal(g1[:, :], gden[:, :]))
            link(dve.tensor_tensor(g2[:, :], ge[:, :], g1[:, :], ALU.mult))

            with dve.Fori(0, ITERS) as it:
                for k in range(UNROLL):
                    hidden_of(0, it * UNROLL + k, k)
            most = most_tokens(dve)
            with dve.If(most > CAP):
                with dve.Fori(1, ROUNDS) as rnd:
                    dve.wait_ge(rank_ready, rnd + 1)
                    dve.tensor_scalar(later[:, :, :], rank[:, :, :], 0.0, float((E - 1) * CAP), ALU.is_ge,
                                      ALU.mult).then_inc(later_ready, 1)
                    dve.wait_ge(later_ready, 2 * rnd - 1)
                    dve.tensor_tensor(ypos[:, :, :], ypos[:, :, :], later[:, :, :], ALU.add).then_inc(later_ready, 1)
                    dve.wait_ge(later_ready, 2 * rnd)
                    dve.wait_ge(tok_now_ready, rnd * (E // GSLOTS))
                    lists(rnd)
                    with dve.Fori(0, ITERS) as it:
                        for k in range(UNROLL):
                            hidden_of(rnd, it * UNROLL + k, k)
                dve.tensor_copy(ypos_i[:, :, :], ypos[:, :, :]).then_inc(ypos_ready, 1)
            for k, (g, dst) in enumerate(((g1, gmat2), (g2, gmat))):
                link(dve.tensor_tensor(dst[:, :, :], oh[:, k, :, :], g[:, :].unsqueeze(2).to_broadcast([P, NT, E]), ALU.mult))
            dve.tensor_tensor(gmat[:, :, :], gmat[:, :, :], gmat2[:, :, :], ALU.add).then_inc(gmat_ready, 1)
            for c in range(NCH):
                k = len(chunk_tiles(c))
                dve.wait_ge(bias_ps, c + 1)
                for t in chunk_tiles(c):
                    m = rows_of(t)
                    dve.tensor_tensor(x1[0:m, t, :], x1[0:m, t, :], banks[c][0:m, t % TPC * P:(t % TPC + 1) * P],
                                      ALU.add).then_inc(bias_done, 1)
            for t in range(NT):
                m = rows_of(t)
                dve.wait_ge(bias_done, t + 1)
                for k, g in enumerate((g1, g2)):
                    n = 2 * t + k
                    dve.wait_ge(yg_in[n % 8], 16 * (n // 8 + 1))
                    ins = dve.scalar_tensor_tensor(x1[0:m, t, :], yg[0:m, n % 8, :], g[0:m, t:t + 1], x1[0:m, t, :],
                                                   ALU.mult, ALU.add)
                    if k == 0:
                        link(ins)
                    else:
                        ins.then_inc(row_done, 1)


_INS = ['x', 'adj', 'L0_gnn_a', 'L0_ffn_Wr', 'L0_ffn_br', 'L0_ffn_W1', 'L0_ffn_b1', 'L0_ffn_W2', 'L0_ffn_b2']


def kernel(**inputs):
    import numpy as _np
    import concourse.bacc as _bacc
    from concourse import mybir as _mybir
    from concourse.bass_utils import run_bass_kernel_spmd as _run

    nc = _bacc.Bacc("TRN2", target_bir_lowering=False, num_devices=1)
    arrays, args = {}, []
    for name in _INS:
        v = _np.ascontiguousarray(inputs[name])
        arrays[f"in_{name}_dram"] = v
        args.append(nc.dram_tensor(f"in_{name}_dram", v.shape, _mybir.dt.from_np(v.dtype), kind="ExternalInput").ap())
    shape = tuple(inputs["x"].shape)
    args.append(nc.dram_tensor("out_0_dram", shape, _mybir.dt.float32, kind="ExternalOutput").ap())
    gat_moe(nc, *args)
    r = _run(nc, [arrays], core_ids=[0])
    return r.results[0]["out_0_dram"]
```

```python
from contextlib import ExitStack

import concourse.bass as bass
from concourse import mybir

F32 = mybir.dt.float32
BF16 = mybir.dt.bfloat16
I32 = mybir.dt.int32
U32 = mybir.dt.uint32
ALU = mybir.AluOpType
ACT = mybir.ActivationFunctionType
AX_X = mybir.AxisListType.X

P = 128
BANK = 512
BIG = 2.0 ** 53
ALPHA = 0.2
EPS = 1e-5
CAP = 88
UNROLL = 16
AHEAD = 2 * UNROLL - 2
GSLOTS = 8
WINDOWS = 4
FLUSH_AT = (9, 12, 15, 18, 21)
FLUSHES = len(FLUSH_AT)


class Steps:

    def __init__(self, eng, sem):
        self.eng, self.sem, self.n = eng, sem, 0

    def clear(self):
        self.eng.sem_clear(self.sem)
        self.n = 0

    def tick(self, ins):
        self.n += 1
        ins.then_inc(self.sem, 1)
        return self.n

    def after(self, n):
        self.eng.wait_ge(self.sem, n)

    def link(self, ins):
        self.after(self.tick(ins))


def gat_moe(nc, x, adj, a, Wr, br, W1, b1, W2, b2, out):
    N, D = x.shape
    E, _, H = W1.shape
    HC = H // P
    NT = -(-N // P)
    LAST = N - P * (NT - 1)
    NP = NT * P
    R = 2 * N
    RT = -(-R // P)
    RLAST = R - P * (RT - 1)
    WMAX = -(-N // CAP)
    ITERS = E // UNROLL
    NCH = -(-NP // BANK)
    TPC = BANK // P
    ACT_TILES = 5
    assert D == P and H == 2 * P and NT % 2 == 1 and E % UNROLL == 0 and NCH == 3

    ctx = ExitStack()
    with ctx:
        def sb(name, shape, dt=F32):
            return ctx.enter_context(nc.sbuf_tensor(name, shape, dt))

        def sem(name):
            return ctx.enter_context(nc.semaphore(name))

        banks = [ctx.enter_context(nc.psum_tensor(f"bank{i}", [P, BANK], F32)) for i in range(8)]
        pt_bank, o_bank, xh2T_bank, c_bank = banks[0:3], banks[4:6], banks[6], banks[7]
        rp_bank, off_bank = banks[6], banks[3]
        rank_banks = ((banks[2], 0, 8), (banks[1], 8, NT))
        gT_banks, bias_banks = (banks[0], banks[4], banks[0]), (banks[5], banks[6], banks[4])
        x_bank, h_bank, y_bank, back_bank = banks[0:2], banks[2:4], banks[4:6], banks[6:8]

        xh2_dram = nc.dram_tensor("xh2_rows", [N, D], F32, kind="Internal").ap()
        y_dram = nc.dram_tensor("expert_rows", [2 * NP, D], F32, kind="Internal").ap()

        x_sb = sb("x_sb", [P, NT, D])
        a2_sb = sb("a2_sb", [P, 1])
        a1_bc = sb("a1_bc", [P, D])
        w1_terms = sb("w1_terms", [P, 2, D])
        Wr_sb = sb("Wr_sb", [P, E])
        br_bc = sb("br_bc", [P, E])
        b1_sb = sb("b1_sb", [E, H])
        b2_sb = sb("b2_sb", [E, D])
        identf = sb("identf", [P, P])
        before = sb("before", [P, P], BF16)
        ones_bf = sb("ones_bf", [P, P], BF16)
        ones_f = sb("ones_f", [P, P])
        iota_e = sb("iota_e", [P, E])
        iota_p = sb("iota_p", [P, P])
        tok_in_tile = sb("tok_in_tile", [P, 1])
        tok_tile = sb("tok_tile", [P, 2, NT])
        nowhere = sb("nowhere", [P, 2, NT])
        need = sb("need", [1, E])
        neg_half = sb("neg_half", [P, NT])
        bn = sb("bn", [P, NT, 6])
        mv = sb("mv", [P, NT, 2])
        ve = sb("ve", [P, NT])
        rstd = sb("rstd", [P, NT])
        hx = sb("hx", [P, NT, D + 1])
        hT = sb("hT", [P, NP])
        a2_bc = sb("a2_bc", [P, P])
        aw2_bc = sb("aw2_bc", [P, NP])
        w1s = sb("w1s", [P, NT])
        adj_sb = sb("adj_sb", [P, 2, N], I32)
        mask = sb("mask", [P, 2, N], BF16)
        low = sb("low", [P, 2, N])
        relu_s = sb("relu_s", [P, 2, NP])
        soft = sb("soft", [P, 2, NP])
        zmin = sb("zmin", [P, 2])
        pT = sb("pT", [P, 2, NT, P])
        rden = sb("rden", [P, 2])
        x1 = sb("x1", [P, NT, D])
        bn2 = sb("bn2", [P, 2, 6])
        mv2 = sb("mv2", [P, 2, 2])
        ve2 = sb("ve2", [P, 2])
        rstd2 = sb("rstd2", [P, 2])
        xh2 = sb("xh2", [P, 2, D])
        xh2T = sb("xh2T", [P, 2, P])
        logit = sb("logit", [P, NT, E])
        top8 = sb("top8", [P, NT, 8])
        idx8 = sb("idx8", [P, NT, 8], U32)
        exp2 = sb("exp2", [P, 2, NT])
        oh = sb("oh", [P, 2, NT, E], BF16)
        less = sb("less", [P, 2, NT, E], BF16)
        ohcum = sb("ohcum", [P, NT, E], BF16)
        ohsum = sb("ohsum", [P, NT, E], BF16)
        off_sb = sb("off_sb", [P, E])
        pos = sb("pos", [P, 2, NT])
        pos_i = sb("pos_i", [P, 2, NT], I32)
        pos_tile = sb("pos_tile", [P, 2, NT], I32)
        pos_col = sb("pos_col", [P, 2, NT], I32)
        minus_col = sb("minus_col", [P, NT])
        tile_oh = sb("tile_oh", [P, 2, NT, RT], BF16)
        tok_oh = sb("tok_oh", [P, 2, NT, 2, RT], BF16)
        col_oh = sb("col_oh", [P, 2, NT, P], BF16)
        dst_parts = sb("dst_parts", [P, 2, RT])
        dst_f = sb("dst_f", [P, RT])
        second = sb("second", [P, RT])
        src_i = sb("src_i", [P, RT], I32)
        dst_i = sb("dst_i", [P, RT], I32)
        offs = sb("offs", [1, E + 1])
        off_i = sb("off_i", [1, E], I32)
        last_off_i = sb("last_off_i", [1, E + 2], I32)
        guard = sb("guard", [1, 2 * E])
        most = sb("most", [1, 1])
        general_i = sb("general_i", [1, 1], I32)
        window_at = sb("window_at", [1, E, WMAX])
        window_i = sb("window_i", [1, E * WMAX], I32)
        ge = sb("ge", [P, NT])
        gden = sb("gden", [P, NT])
        gate = sb("gate", [P, 2, NT])
        gate_rest = sb("gate_rest", [P, 2, NT])
        gate_parts = sb("gate_parts", [P, 3, 2, NT], BF16)
        gate_oh = sb("gate_oh", [P, 2, NT, 3, RT], BF16)
        sorted_parts = sb("sorted_parts", [P, 3, RT])
        sorted_gate = sb("sorted_gate", [P, RT])
        xg = sb("xg", [P, GSLOTS, D])
        xT = sb("xT", [P, WINDOWS, CAP])
        back_in = sb("back_in", [P, 2, P])
        w1_ring = sb("w1_ring", [P, AHEAD, H])
        w2_ring = sb("w2_ring", [P, AHEAD, HC, D])
        b1T = sb("b1T", [P, HC, E])
        hidden = sb("hidden", [P, 4, HC, CAP])
        xT_sorted = pT.rearrange("p a t i -> p (a t i)")
        yT_sorted = soft.rearrange("p a j -> p (a j)")
        y_rows = relu_s.rearrange("p a j -> p (a j)")[:, 0:RT * D].rearrange("p (t d) -> p t d", d=D)
        y2 = pT
        low_room = low.rearrange("p a j -> p (a j)")
        rowno = low_room[:, 0:NT * E].rearrange("p (t e) -> p t e", e=E)
        picked = low_room[:, NT * E:3 * NT * E].rearrange("p (k t e) -> p k t e", k=2, e=E)
        gmat = hT[:, 0:NT * E].rearrange("p (t e) -> p t e", e=E)
        squares = hT[:, NT * E:NT * E + ACT_TILES * P].rearrange("p (t c) -> p t c", c=P)
        gmat2 = xT_sorted[:, 0:NT * E].rearrange("p (t e) -> p t e", e=E)
        gT = aw2_bc[0:E, :]

        x_in = [sem(f"x_in{i}") for i in range(NCH)]
        small_in = sem("small_in")
        a1_in = sem("a1_in")
        a2_in = sem("a2_in")
        adj_in = [sem(f"adj_in{i}") for i in range(2)]
        ident_ready = sem("ident_ready")
        filled = sem("filled")
        stats_ready = sem("stats_ready")
        rstd_ready = sem("rstd_ready")
        h_ready = sem("h_ready")
        hT_ps = sem("hT_ps")
        hT_ready = sem("hT_ready")
        w1_ready = sem("w1_ready")
        w2bc_ps = sem("w2bc_ps")
        w2bc_ready = sem("w2bc_ready")
        a2_ready = sem("a2_ready")
        b1T_ps = sem("b1T_ps")
        b1T_ready = sem("b1T_ready")
        mask_ready = sem("mask_ready")
        low_ready = sem("low_ready")
        first_low = sem("first_low")
        relu_ready = sem("relu_ready")
        z_ready = sem("z_ready")
        p_ready = sem("p_ready")
        pT_ps = sem("pT_ps")
        pT_act = sem("pT_act")
        pT_dve = sem("pT_dve")
        o_ps = sem("o_ps")
        xh2_ready = sem("xh2_ready")
        xh2T_ps = sem("xh2T_ps")
        xh2T_ready = sem("xh2T_ready")
        logit_ps = sem("logit_ps")
        logit_ready = sem("logit_ready")
        oh_ready = sem("oh_ready")
        ohcum_ready = sem("ohcum_ready")
        xh2_out = [sem(f"xh2_out{i}") for i in range(2)]
        zeros_ready = sem("zeros_ready")
        mv2_ready = sem("mv2_ready")
        rstd2_ready = sem("rstd2_ready")
        rank_ps = sem("rank_ps")
        diff_ready = sem("diff_ready")
        gexp_ready = sem("gexp_ready")
        gates_ready = sem("gates_ready")
        gmat2_ready = sem("gmat2_ready")
        gate_parts_ready = sem("gate_parts_ready")
        tile_oh_ready = sem("tile_oh_ready")
        tok_oh_ready = sem("tok_oh_ready")
        col_ready = sem("col_ready")
        squares_ready = sem("squares_ready")
        act_col_oh_ready = sem("act_col_oh_ready")
        gate_oh_ready = sem("gate_oh_ready")
        gates_ps = sem("gates_ps")
        sorted_gate_ready = sem("sorted_gate_ready")
        picked_ready = sem("picked_ready")
        off_ps = sem("off_ps")
        off_ready = sem("off_ready")
        positions_ready = sem("positions_ready")
        guard_ready = sem("guard_ready")
        pos_oh_ready = sem("pos_oh_ready")
        dst_ps = sem("dst_ps")
        src_ready = sem("src_ready")
        dst_ready = sem("dst_ready")
        general_ready = sem("general_ready")
        windows_made = sem("windows_made")
        windows_ready = sem("windows_ready")
        gmat_ready = sem("gmat_ready")
        xg_in = [sem(f"xg_in{i}") for i in range(GSLOTS)]
        w_in = [sem(f"w_in{i}") for i in range(AHEAD // 2)]
        xT_ps = sem("xT_ps")
        xT_ready = sem("xT_ready")
        window_ready = sem("window_ready")
        h_ps = sem("h_ps")
        hid_ready = sem("hid_ready")
        y_ps = sem("y_ps")
        yT_ready = sem("yT_ready")
        staged = sem("staged")
        back_ps = sem("back_ps")
        rows_ready = sem("rows_ready")
        y_out = sem("y_out")
        g_w_in = [sem(f"g_w_in{i}") for i in range(2)]
        g_w_free = sem("g_w_free")
        g_window = sem("g_window")
        g_h_ps = sem("g_h_ps")
        g_hid = sem("g_hid")
        g_y_ps = sem("g_y_ps")
        g_yT = sem("g_yT")
        gT_ps = sem("gT_ps")
        gT_ready = sem("gT_ready")
        bias_ps = sem("bias_ps")
        bias_done = sem("bias_done")
        y2_in = [sem(f"y2_in{i}") for i in range(NCH + 1)]
        sums_done = [sem(f"sums_done{i}") for i in range(NCH + 1)]
        out_written = sem("out_written")
        dve_link = sem("dve_link")
        pool_link = sem("pool_link")
        const_made = sem("const_made")
        passed = sem("passed")

        ZEROS = 5
        LOADS = 4
        STEADY0, STEADY1 = 3, 7
        rows_of = lambda t: P if isinstance(t, int) and t < NT - 1 or not isinstance(t, int) else LAST

        SLOPE = -(-FLUSHES * P // UNROLL)
        SLACK = min(SLOPE * (s - 3) - P * (j + 1) for j, s in enumerate(FLUSH_AT))
        CHOICES = {8: slice(0, 5), 9: slice(5, 8), 11: slice(8, 10), 12: slice(10, 11)}
        assert NT == 11
        CONST = 12
        BIASED = NCH + 1
        PARTS = ((slice(0, 2 * TPC), range(2)), (slice(2 * TPC, NT), range(2, NCH)))
        POOL_SUM = 1
        SUMS = [(0, 5), (5, 7), (7, NT - 1), (NT - 1, NT)]

        def chunk_tiles(c):
            return list(range(c * TPC, min((c + 1) * TPC, NT)))

        def attention_steps(eng, step, steps=None):
            for t in range(-3, STEADY0):
                step(t, t % 2)
            with eng.Fori(STEADY0 // 2, STEADY1 // 2) as i:
                if steps:
                    steps.clear()
                step(i * 2 + 1, 1)
                step(i * 2 + 2, 0)
            if steps:
                steps.clear()
            for t in range(STEADY1, NT + 2):
                step(t, t % 2)

        def has(u):
            return not isinstance(u, int) or 0 <= u < NT

        def needs(eng, semaphore, value):
            if not isinstance(value, int) or value > 0:
                eng.wait_ge(semaphore, value)

        def wait_apart(eng, semaphore, value):
            eng.wait_ge(semaphore, value)
            if not isinstance(value, int):
                eng.sem_inc(passed, 1)

        def tiles3(buf, k, n):
            return buf[:, 0:k * P].rearrange("p (t c) -> p t c", c=P)[:, :, 0:n]

        def loads16(u, q):
            return (u - q) * 8 + 16

        def take_general(eng):
            eng.wait_ge(general_ready, 1)
            return eng.value_load(general_i[0:1, 0:1], min_val=0, max_val=1)

        class Positions:

            def __init__(self, eng):
                self.eng, self.loads, self.values = eng, 0, []

            def load(self, table, n=UNROLL):
                registers = [self.eng.alloc_register(f"first_{self.loads}_{i}") for i in range(n)]
                self.loads += 1
                self.eng.load(registers, table)
                self.values = [self.eng.snap(r, donate=True, min_val=0, max_val=R) for r in registers]

            def __getitem__(self, k):
                return self.values[k]

        def tiles_for(e):
            return min(-(-CAP * (e + 1) // P), RT)

        def tiles_ahead(e):
            return min(tiles_for(e + 3), e + 3)

        def expert_steps(step):
            def run(eng):
                for e in range(2 * UNROLL):
                    step(e, e % UNROLL, e // UNROLL)
                with eng.Fori(2, ITERS) as it:
                    for k in range(UNROLL):
                        step(it * UNROLL + k, k, it)
                step(E, 0, ITERS)
                step(E + 1, 1, ITERS)
            return run

        assert tiles_for(2 * UNROLL - 1) == RT and FLUSHES * (ITERS - 1) < RT

        def flush_tile(e, k, it):
            back = k + UNROLL in FLUSH_AT
            if not back and k not in FLUSH_AT:
                return None
            j = FLUSH_AT.index(k + UNROLL * back)
            m = (it - back) * FLUSHES + j
            return None if isinstance(e, int) and (m < 0 or e >= E) else (m, j % 2)

        STAGED0 = FLUSHES * 2 - sum(s >= UNROLL for s in FLUSH_AT)
        assert SLOPE * (E - 1) - SLACK >= P * (FLUSHES * (ITERS - 1) + sum(s < UNROLL for s in FLUSH_AT) + 1)
        LEFT = [m for m in range(RT) if m // FLUSHES * UNROLL + FLUSH_AT[m % FLUSHES] >= E]
        rows_of_sorted = lambda m: RLAST if isinstance(m, int) and m == RT - 1 else P

        def by_choice(buf):
            return buf[:, :, :, :].rearrange("p k t m -> p (k t) m")

        def slot_of(e):
            return e if e < AHEAD else e % UNROLL

        def last_in_slot(e):
            return max(f for f in range(e) if slot_of(f) == slot_of(e))

        def loads_in_slot(e):
            return sum(slot_of(f) == slot_of(e) for f in range(e + 1))

        block = ctx.enter_context(nc.Block())

        @block.sync
        def _(sp):
            for c in range(NCH):
                ts = [t for t in chunk_tiles(c) if rows_of(t) == P]
                sp.dma_start(x_sb[:, ts[0]:ts[-1] + 1, :],
                             x[P * ts[0]:P * (ts[-1] + 1), :].rearrange("(t p) d -> p t d", p=P)).then_inc(x_in[c], 16)
                if c == NCH - 1:
                    sp.dma_start(x_sb[0:LAST, NT - 1, :], x[P * (NT - 1):N, :]).then_inc(x_in[c], 16)
            sp.dma_start(adj_sb[:, 0, :], adj[0:P, :]).then_inc(adj_in[0], 16)
            sp.dma_start(adj_sb[:, 1, :], adj[P:2 * P, :]).then_inc(adj_in[1], 16)

            def load_weights(pair, e0):
                sp.dma_start(w1_ring[:, 2 * pair:2 * pair + 2, :],
                             W1[bass.ds(e0, 2), :, :].rearrange("e p h -> p e h")).then_inc(w_in[pair], 16)
                sp.dma_start(w2_ring[:, 2 * pair:2 * pair + 2, :, :].rearrange("p e c d -> p (e c) d"),
                             W2[bass.ds(e0, 2), :, :].rearrange("e (c p) d -> p (e c) d", p=P)).then_inc(w_in[pair], 16)

            def step(t, par):
                q = (par + 1) % 2
                if has(t + 3) and not (isinstance(t, int) and t + 3 < 2):
                    n = rows_of(t + 3)
                    sp.wait_ge(mask_ready, t + 2)
                    sp.dma_start(adj_sb[0:n, q, :], adj[bass.ds((t + 3) * P, n), :]).then_inc(adj_in[q], 16)
                if isinstance(t, int) and (-1 <= t < STEADY0 or STEADY1 <= t < STEADY1 + 4):
                    first = 2 * (t + 1 if t < STEADY0 else STEADY0 + 1 + t - STEADY1)
                    for k in range(first, min(first + 2, AHEAD // 2)):
                        load_weights(k, 2 * k)
                if has(t - 2):
                    sp.wait_ge(xh2_ready, t - 1)
                    n = rows_of(t - 2)
                    sp.dma_start(xh2_dram[bass.ds((t - 2) * P, n), :], xh2[0:n, par, :]).then_inc(xh2_out[par], 16)

            attention_steps(sp, step)

            general = take_general(sp)
            with sp.If(general > 0):
                for k in range(AHEAD // 2):
                    sp.wait_ge(w_in[k], 32)
                with sp.Fori(0, E // 2) as i:
                    for u in range(2):
                        sp.wait_ge(g_w_free, i * 2 + u + 1)
                        sp.dma_start(w1_ring[:, u:u + 1, :],
                                     W1[bass.ds(i * 2 + u, 1), :, :].rearrange("e p h -> p e h")).then_inc(g_w_in[u], 16)
                        sp.dma_start(w2_ring[:, u:u + 1, :, :].rearrange("p e c d -> p (e c) d"),
                                     W2[bass.ds(i * 2 + u, 1), :, :].rearrange("e (c p) d -> p (e c) d", p=P)
                                     ).then_inc(g_w_in[u], 16)
            with sp.Else():
                for e in sorted(range(AHEAD, E, 2), key=last_in_slot):
                    sp.wait_ge(y_ps, last_in_slot(e) + 2)
                    load_weights(slot_of(e) // 2, e)
            sp.wait_ge(y_out, 16 * RT)
            for g, (t0, t1) in enumerate(SUMS):
                n = rows_of(t0)
                for k in range(2):
                    sp.dma_start(y2[0:n, k, t0:t1, :], y_dram.rearrange("(k t p) d -> p k t d", k=2, p=P)[0:n, k, t0:t1, :]
                                 ).then_inc(y2_in[g], 16)
            for g, (t0, t1) in enumerate(SUMS):
                sp.wait_ge(sums_done[g], 1)
                n = rows_of(t0)
                sp.dma_start(out[t0 * P:t0 * P + (t1 - t0 - 1) * P + n, :].rearrange("(t p) d -> p t d", p=n),
                             x1[0:n, t0:t1, :]).then_inc(out_written, 16)
            sp.wait_ge(out_written, 16 * len(SUMS))

        @block.gpsimd
        def _(pool):
            steps = Steps(pool, pool_link)
            link = steps.link
            pool.memset(identf[:, :], 0.0).then_inc(filled, 1)
            pool.memset(ones_f[:, :], 1.0).then_inc(filled, 1)
            pool.memset(neg_half[:, :], -0.5).then_inc(filled, 1)
            pool.wait_ge(filled, 3)
            pool.affine_select(out=identf[:, :], in_=identf[:, :], compare_op=ALU.not_equal, fill=1.0, base=0,
                               pattern=[[-1, P]], channel_multiplier=1).then_inc(ident_ready, 1)
            for c in range(NCH):
                ts = slice(c * TPC, min((c + 1) * TPC, NT))
                pool.wait_ge(stats_ready, c + 1)
                link(pool.tensor_scalar(ve[:, ts], mv[:, ts, 1], EPS, None, ALU.add))
                pool.tensor_tensor(rstd[:, ts], ve[:, ts], neg_half[:, ts], ALU.pow).then_inc(rstd_ready, 1)
            pool.wait_ge(w2bc_ready, NCH)

            def gate_matrix(part):
                ts = PARTS[part][0]
                n = ts.stop - ts.start
                pool.wait_ge(gates_ready, 2 * part + 2)
                link(pool.tensor_tensor(gmat[:, ts, :], oh[:, 0, ts, :], gate[:, 0, ts].unsqueeze(2).to_broadcast([P, n, E]),
                                        ALU.mult))
                pool.wait_ge(gmat2_ready, part + 1)
                pool.tensor_tensor(gmat[:, ts, :], gmat[:, ts, :], gmat2[:, ts, :], ALU.add).then_inc(gmat_ready, 1)

            def constants():
                pool.memset(ones_bf[:, :], 1.0).then_inc(const_made, 1)
                pool.memset(oh[:, :, NT - 1, :], 0.0).then_inc(const_made, 1)
                pool.memset(less[:, :, NT - 1, :], 0.0).then_inc(const_made, 1)
                pool.memset(top8[:, NT - 1, :], 0.0).then_inc(const_made, 1)
                pool.memset(ohcum[:, 0, :], 0.0).then_inc(const_made, 1)
                pool.iota(iota_e[:, :], [[1, E]], base=0, channel_multiplier=0,
                          allow_small_or_imprecise_dtypes=True).then_inc(const_made, 1)
                pool.memset(nowhere[:, :, :], 0.0).then_inc(filled, 1)
                pool.wait_ge(const_made, 6)
                pool.wait_ge(filled, 4)
                pool.affine_select(out=before[:, :], in_=ones_bf[:, :], compare_op=ALU.is_gt, fill=0.0, base=0,
                                   pattern=[[1, P]], channel_multiplier=-1).then_inc(const_made, 1)

            def more_constants():
                pool.affine_select(out=nowhere[:, :, :], in_=nowhere[:, :, :], compare_op=ALU.is_gt, fill=float(P * P),
                                   base=N, pattern=[[0, 2], [-P, NT]], channel_multiplier=-1).then_inc(const_made, 1)
                pool.iota(iota_p[:, :], [[1, P]], base=0, channel_multiplier=0,
                          allow_small_or_imprecise_dtypes=True).then_inc(const_made, 1)
                pool.iota(tok_in_tile[:, :], [[0, 1]], base=0, channel_multiplier=1,
                          allow_small_or_imprecise_dtypes=True).then_inc(const_made, 1)
                pool.iota(tok_tile[:, :, :], [[NP, 2], [P, NT]], base=0, channel_multiplier=0,
                          allow_small_or_imprecise_dtypes=True).then_inc(const_made, 1)
                pool.iota(need[:, :], [[SLOPE, E]], base=-SLACK, channel_multiplier=0,
                          allow_small_or_imprecise_dtypes=True).then_inc(const_made, 1)

            def step(t, par):
                q = (par + 1) % 2
                if has(t + 2) and not (isinstance(t, int) and t == -2):
                    n = rows_of(t + 2)
                    wait_apart(pool, mask_ready, t + 3)
                    needs(pool, z_ready, t + 1)
                    if not isinstance(t, int):
                        pool.sem_inc(passed, 1)
                    pool.tensor_tensor(low[0:n, par, :], mask[0:n, par, :], aw2_bc[0:n, 0:N], ALU.add).then_inc(low_ready, 1)
                if isinstance(t, int) and t == -2:
                    pool.wait_ge(first_low, 1)
                    pool.sem_inc(low_ready, 1)
                if has(t - 1):
                    n = rows_of(t - 1)
                    wait_apart(pool, mv2_ready, t)
                    link(pool.tensor_scalar(ve2[0:n, q:q + 1], mv2[0:n, q, 1:2], EPS, None, ALU.add))
                    pool.tensor_tensor(rstd2[0:n, q:q + 1], ve2[0:n, q:q + 1], neg_half[0:n, 0:1],
                                       ALU.pow).then_inc(rstd2_ready, 1)
                if isinstance(t, int):
                    if t == NT + 1:
                        gate_matrix(0)
                    if t == STEADY1:
                        constants()
                    if t == NT - 2:
                        more_constants()
                    if t in CHOICES and CHOICES[t].stop < NT:
                        ts = CHOICES[t]
                        pool.wait_ge(oh_ready, ts.stop)
                        link(pool.tensor_tensor(ohsum[:, ts, :], oh[:, 0, ts, :], oh[:, 1, ts, :], ALU.add))
                        for u in range(ts.start, ts.stop):
                            if u:
                                pool.wait_ge(ohcum_ready, u)
                            pool.tensor_tensor(ohcum[:, u + 1, :], ohcum[:, u, :], ohsum[:, u, :],
                                               ALU.add).then_inc(ohcum_ready, 1)

            attention_steps(pool, step, steps)

            for par, k in ((0, (NT + 1) // 2), (1, NT // 2)):
                pool.wait_ge(xh2_out[par], 16 * k)
            pool.memset(offs[:, E:E + 1], float(R)).then_inc(filled, 1)
            pool.memset(last_off_i[:, 0:2], 0).then_inc(filled, 1)
            pool.wait_ge(off_ready, 1)
            pool.tensor_copy(offs[:, 0:E], off_sb[0:1, :]).then_inc(filled, 1)
            pool.wait_ge(filled, 7)
            pool.tensor_copy(off_i[:, :], offs[:, 0:E]).then_inc(positions_ready, 1)
            pool.tensor_copy(last_off_i[:, 2:E + 2], offs[:, 0:E]).then_inc(positions_ready, 1)
            link(pool.tensor_tensor(guard[:, 0:E], offs[:, 1:E + 1], offs[:, 0:E], ALU.subtract))
            pool.tensor_tensor(guard[:, E:2 * E], need[:, :], offs[:, 0:E], ALU.subtract).then_inc(guard_ready, 1)
            pool.tensor_scalar(guard[:, 0:E], guard[:, 0:E], -float(CAP), None, ALU.add).then_inc(guard_ready, 1)
            pool.wait_ge(gates_ready, 4)
            link(pool.tensor_copy(gate_parts[:, 0, :, :], gate[:, :, :]))
            link(pool.tensor_tensor(gate_rest[:, :, :], gate[:, :, :], gate_parts[:, 0, :, :], ALU.subtract))
            link(pool.tensor_copy(gate_parts[:, 1, :, :], gate_rest[:, :, :]))
            pool.tensor_tensor(gate_parts[:, 2, :, :], gate_rest[:, :, :], gate_parts[:, 1, :, :],
                               ALU.subtract).then_inc(gate_parts_ready, 1)
            gate_matrix(1)
            pool.wait_ge(tile_oh_ready, 1)
            pool.tensor_tensor(tok_oh[:, :, :, 1, :].rearrange("p k t m -> p (k t) m"), by_choice(tile_oh),
                               tok_tile[:, :, :].rearrange("p k t -> p (k t)").unsqueeze(2).to_broadcast([P, 2 * NT, RT]),
                               ALU.mult).then_inc(tok_oh_ready, 1)
            pool.wait_ge(src_ready, 1)
            for m in range(RT):
                if m >= GSLOTS:
                    pool.wait_ge(xT_ps, m - GSLOTS + 1)
                pool.indirect_dma_start(xg[:, m % GSLOTS, :], None, xh2_dram,
                                        bass.IndirectOffsetOnAxis(ap=src_i[:, m:m + 1], axis=0)
                                        ).then_inc(xg_in[m % GSLOTS], 16)
            pool.wait_ge(dst_ready, 1)
            for m in range(RT):
                n = rows_of_sorted(m)
                pool.wait_ge(rows_ready, m + 1)
                pool.indirect_dma_start(y_dram, bass.IndirectOffsetOnAxis(ap=dst_i[0:n, m:m + 1], axis=0),
                                        y_rows[0:n, m, :], None).then_inc(y_out, 16)
            t0, t1 = SUMS[POOL_SUM]
            pool.wait_ge(bias_done, BIASED)
            pool.wait_ge(y2_in[POOL_SUM], 32)
            link(pool.tensor_tensor(x1[:, t0:t1, :], x1[:, t0:t1, :], y2[:, 0, t0:t1, :], ALU.add))
            pool.tensor_tensor(x1[:, t0:t1, :], x1[:, t0:t1, :], y2[:, 1, t0:t1, :], ALU.add).then_inc(sums_done[POOL_SUM], 1)

        @block.scalar
        def _(act):
            act.dma_start(a2_sb[:, :], a[D:2 * D, :], allow_slow_non_contiguous=True).then_inc(a2_in, 16)
            act.dma_start(a1_bc[:, :], a[0:D, :].rearrange("d o -> o d").to_broadcast([P, D])).then_inc(a1_in, 16)
            act.dma_start(Wr_sb[:, :], Wr).then_inc(small_in, 16)
            act.dma_start(br_bc[:, :], br.unsqueeze(0).to_broadcast([P, E])).then_inc(small_in, 16)
            act.dma_start(b1_sb[:, :], b1).then_inc(small_in, 16)
            act.dma_start(b2_sb[:, :], b2).then_inc(small_in, 16)
            for c in range(NCH):
                w = min(BANK, NP - c * BANK)
                act.wait_ge(hT_ps, c + 1)
                act.copy(hT[:, c * BANK:c * BANK + w], banks[c][:, 0:w]).then_inc(hT_ready, 1)
            for c in range(NCH):
                w = min(BANK, NP - c * BANK)
                act.wait_ge(w2bc_ps, c + 1)
                act.copy(aw2_bc[:, c * BANK:c * BANK + w], banks[3 + c][:, 0:w]).then_inc(w2bc_ready, 1)
                if c == 0:
                    act.wait_ge(w1_ready, NT)
                act.wait_ge(w2bc_ready, c + 1)
                end = min(c * BANK + w, N)
                last = act.activation(relu_s[:, 0, c * BANK:end], aw2_bc[:, c * BANK:end], ACT.Relu, bias=w1s[:, 0:1],
                                      scale=(1.0 - ALPHA) / ALPHA)
            last.then_inc(relu_ready, 1)

            def gate_exponent(part):
                ts = PARTS[part][0]
                act.wait_ge(diff_ready, part + 1)
                act.activation(ge[:, ts], gden[:, ts], ACT.Exp).then_inc(gexp_ready, 1)

            def second_gates(part):
                ts = PARTS[part][0]
                act.wait_ge(gates_ready, 2 * part + 2)
                for t in range(ts.start, ts.stop):
                    last = act.activation(gmat2[:, t, :], oh[:, 1, t, :], ACT.Copy, scale=gate[:, 1, t:t + 1])
                last.then_inc(gmat2_ready, 1)

            def transposed_gates(part):
                for c in PARTS[part][1]:
                    w = min(BANK, NP - c * BANK)
                    act.wait_ge(gT_ps, c + 1)
                    act.copy(gT[:, c * BANK:c * BANK + w], gT_banks[c][0:E, 0:w]).then_inc(gT_ready, 1)

            def step(t, par):
                n = rows_of(t)
                q = (par + 1) % 2

                def transposed(c):
                    k = len(chunk_tiles(c))
                    act.wait_ge(pT_ps, 3 * t + c + 1)
                    needs(act, o_ps, t - 1)
                    act.copy(pT[:, par, c * TPC:c * TPC + k, 0:n], tiles3(pt_bank[c], k, n)).then_inc(pT_act, 1)

                if isinstance(t, int) and t == NT + 1:
                    gate_exponent(0)
                if has(t):
                    transposed(0)
                if has(t + 2) and not (isinstance(t, int) and t == -2):
                    m = rows_of(t + 2)
                    needs(act, z_ready, t + 1)
                    w1 = w1s[0:m, t + 2:t + 3] if isinstance(t, int) else w1s[:, bass.ds(t + 2, 1)]
                    act.activation(relu_s[0:m, par, 0:N], aw2_bc[0:m, 0:N], ACT.Relu, bias=w1,
                                   scale=(1.0 - ALPHA) / ALPHA).then_inc(relu_ready, 1)
                if has(t):
                    transposed(2)
                if has(t - 2):
                    m = rows_of(t - 2)
                    act.wait_ge(xh2T_ps, t - 1)
                    act.copy(xh2T[:, par, 0:m], xh2T_bank[:, 0:m]).then_inc(xh2T_ready, 1)
                if has(t + 1):
                    m = rows_of(t + 1)
                    act.wait_ge(z_ready, t + 2)
                    act.activation(soft[0:m, q, 0:N], soft[0:m, q, 0:N], ACT.Exp, bias=zmin[0:m, q:q + 1],
                                   scale=-1.0).then_inc(p_ready, 1)
                if isinstance(t, int) and t == NT + 1:
                    second_gates(0)
                if isinstance(t, int) and t == -1:
                    act.wait_ge(b1T_ps, 1)
                    act.copy(b1T[:, :, :], c_bank[:, 0:HC * E].rearrange("p (c e) -> p c e", c=HC)).then_inc(b1T_ready, 1)

            attention_steps(act, step)
            gate_exponent(1)
            transposed_gates(0)
            second_gates(1)
            transposed_gates(1)
            act.wait_ge(col_ready, 1)
            for i in range(ACT_TILES):
                t = NT - ACT_TILES + i
                last = act.activation(squares[:, i, :], iota_p[:, :], ACT.Square, bias=minus_col[:, t:t + 1])
            last.then_inc(squares_ready, 1)
            act.wait_ge(squares_ready, 1)
            act.activation(col_oh[:, 1, NT - ACT_TILES:NT, :], squares[:, :, :], ACT.Relu, bias=ones_f[:, 0:1],
                           scale=-1.0).then_inc(act_col_oh_ready, 1)

            def tokens(m):
                act.wait_ge(xT_ps, m + 1)
                act.copy(xT_sorted[:, m * P:(m + 1) * P], x_bank[m % 2][:, 0:P]).then_inc(xT_ready, 1)

            def rows(m, b):
                if isinstance(m, int) and m == 0:
                    act.wait_ge(sorted_gate_ready, 1)
                n = rows_of_sorted(m)
                act.wait_ge(back_ps, m + 1)
                dst = y_rows[0:n, m, :] if isinstance(m, int) else y_rows[:, bass.ds(m, 1), :].rearrange("p o d -> p (o d)")
                of_m = sorted_gate[0:n, m:m + 1] if isinstance(m, int) else sorted_gate[:, bass.ds(m, 1)]
                act.activation(dst, back_bank[b][0:n, 0:D], ACT.Copy, scale=of_m).then_inc(rows_ready, 1)

            first = Positions(act)

            def step(e, k, it):
                if k == 0 and not (isinstance(e, int) and e >= E):
                    first.load(off_i[0:1, bass.ds(e, UNROLL)])
                if isinstance(e, int) and e < 2 * UNROLL:
                    for m in range(tiles_for(e - 1) if e else 0, tiles_for(e)):
                        tokens(m)
                if not isinstance(e, int) or e < E:
                    if isinstance(e, int):
                        act.wait_ge(xT_ready, tiles_for(e))
                    if not isinstance(e, int) or e >= WINDOWS:
                        wait_apart(act, h_ps, e - WINDOWS + 1)
                    act.copy(xT[:, k % WINDOWS, :], xT_sorted[:, bass.ds(first[k], CAP)]).then_inc(window_ready, 1)
                if flush := flush_tile(e - 2, (k - 2) % UNROLL, it - (k < 2)):
                    rows(*flush)

            act.wait_ge(positions_ready, 2)
            general = take_general(act)
            with act.If(general > 0):
                for m in range(RT):
                    tokens(m)
                act.wait_ge(windows_ready, 1)
                act.wait_ge(xT_ready, RT)
                act.sem_inc(g_yT, 1)
                with act.Fori(0, E) as e:
                    with act.Fori(0, WMAX) as w:
                        at = act.value_load(window_i[0:1, bass.ds(e * WMAX + w, 1)], min_val=0, max_val=R)
                        wait_apart(act, g_yT, e * WMAX + w + 1)
                        act.copy(xT[:, 0, :], xT_sorted[:, bass.ds(at, CAP)]).then_inc(g_window, 1)
                for m in range(RT):
                    rows(m, m % 2)
            with act.Else():
                expert_steps(step)(act)
                for m in LEFT:
                    rows(m, m % 2)

        @block.tensor
        def _(pe):
            pe.wait_ge(ident_ready, 1)

            def h_transposed(c):
                pe.wait_ge(h_ready, c + 1)
                for t in chunk_tiles(c):
                    last = pe.transpose(banks[c][:, t % TPC * P:(t % TPC + 1) * P], hx[:, t, 0:D], identf[:, :])
                last.then_inc(hT_ps, 1)

            def w2_broadcast(c):
                w = min(BANK, NP - c * BANK)
                pe.wait_ge(hT_ready, c + 1)
                pe.matmul(banks[3 + c][:, 0:w], a2_bc[:, :], hT[:, c * BANK:c * BANK + w],
                          start=True, stop=True).then_inc(w2bc_ps, 1)

            h_transposed(0)
            h_transposed(1)
            pe.wait_ge(a2_ready, 1)
            w2_broadcast(0)
            h_transposed(2)
            w2_broadcast(1)
            w2_broadcast(2)
            pe.wait_ge(small_in, 16 * LOADS)
            for c in range(HC):
                last = pe.transpose(c_bank[:, c * E:(c + 1) * E], b1_sb[:, c * P:(c + 1) * P], identf[0:E, 0:E])
            last.then_inc(b1T_ps, 1)
            pe.wait_ge(b1T_ready, 1)
            pe.wait_ge(zeros_ready, ZEROS)

            def step(t, par):
                n = rows_of(t)

                def transpose_p(c):
                    if c == 0:
                        pe.wait_ge(p_ready, t + 1)
                    needs(pe, pT_dve if c == 1 else pT_act, (2 * t - 1, t, 2 * t)[c])
                    for j in chunk_tiles(c):
                        o = j % TPC * P
                        last = pe.transpose(pt_bank[c][:, o:o + n], soft[0:n, par, j * P:(j + 1) * P], identf[0:n, 0:n])
                    last.then_inc(pT_ps, 1)

                def weigh(c):
                    pe.wait_ge(pT_dve if c == 1 else pT_act, (2 * t + 1, t + 1, 2 * t + 2)[c])
                    if c == 0:
                        needs(pe, mv2_ready, t - 1)
                    for j in chunk_tiles(c):
                        last = pe.matmul(o_bank[par][0:n, 0:D + 1], pT[:, par, j, 0:n], hx[:, j, :],
                                         start=(j == 0), stop=(j == NT - 1))
                    if c == NCH - 1:
                        last.then_inc(o_ps, 1)

                if has(t):
                    transpose_p(0)
                    transpose_p(1)
                if has(t - 2):
                    m = rows_of(t - 2)
                    pe.wait_ge(xh2_ready, t - 1)
                    needs(pe, xh2T_ready, t - 2)
                    pe.transpose(xh2T_bank[:, 0:m], xh2[0:m, par, :], identf[0:m, 0:m]).then_inc(xh2T_ps, 1)
                if has(t):
                    transpose_p(2)
                    weigh(0)
                    weigh(1)
                if has(t - 2):
                    pe.wait_ge(xh2T_ready, t - 1)
                    needs(pe, logit_ready, t - 2)
                    pe.matmul(c_bank[0:m, 0:E], xh2T[:, par, 0:m], Wr_sb[:, :], start=True, stop=True).then_inc(logit_ps, 1)
                if has(t):
                    weigh(2)

            attention_steps(pe, step)

            def first_positions(ts):
                pe.wait_ge(oh_ready, ts.stop)
                for t in range(ts.start, ts.stop):
                    for k in range(2):
                        last = pe.matmul(off_bank[:, 0:E], ones_bf[:, :], less[:, k, t, :], start=(t == 0 and k == 0),
                                         stop=(t == NT - 1 and k == 1))
                return last

            def ranks(bank, t0, t1):
                w = (t1 - t0) * E
                pe.matmul(bank[:, 0:w], before[:, :], oh[:, 0, t0:t1, :], start=True, stop=False)
                pe.matmul(bank[:, 0:w], before[:, :], oh[:, 1, t0:t1, :], start=False, stop=False)
                return pe.matmul(bank[:, 0:w], ones_bf[:, :], ohcum[:, t0:t1, :], start=False, stop=True)

            def transpose_gates(part):
                pe.wait_ge(gmat_ready, part + 1)
                for c in PARTS[part][1]:
                    for t in chunk_tiles(c):
                        last = pe.transpose(gT_banks[c][0:E, t % TPC * P:(t % TPC + 1) * P], gmat[:, t, :], identf[:, :])
                    last.then_inc(gT_ps, 1)

            def bias_rows(part):
                for c in PARTS[part][1]:
                    pe.wait_ge(gT_ready, c + 1)
                    for t in chunk_tiles(c):
                        last = pe.matmul(bias_banks[c][:, t % TPC * P:(t % TPC + 1) * P], gT[:, t * P:(t + 1) * P],
                                         b2_sb[:, :], start=True, stop=True)
                    last.then_inc(bias_ps, 1)

            pe.wait_ge(const_made, 7)
            for t in sorted(CHOICES)[:-1]:
                first_positions(CHOICES[t])
            pe.wait_ge(ohcum_ready, NT - 1)
            ranks(*rank_banks[0])
            first_positions(slice(NT - 1, NT)).then_inc(off_ps, 1)
            ranks(*rank_banks[1]).then_inc(rank_ps, 1)
            transpose_gates(0)
            bias_rows(0)
            transpose_gates(1)
            pe.wait_ge(tok_oh_ready, 2)
            for n, (k, t) in enumerate((k, t) for k in range(2) for t in range(NT)):
                if t == 0:
                    pe.wait_ge(pos_oh_ready, k + 1)
                if k == 1 and t == NT - ACT_TILES:
                    pe.wait_ge(act_col_oh_ready, 1)
                last = pe.matmul(c_bank[:, 0:2 * RT], col_oh[:, k, t, :], tok_oh[:, k, t, :, :],
                                 start=(n == 0), stop=(n == 2 * NT - 1))
            last.then_inc(dst_ps, 1)
            bias_rows(1)
            general = take_general(pe)
            pe.sem_inc(g_w_free, 2)

            def tokens(m):
                pe.wait_ge(xg_in[m % GSLOTS], 16 * (m // GSLOTS + 1))
                needs(pe, xT_ready, m - 1)
                pe.transpose(x_bank[m % 2][:, 0:P], xg[:, m % GSLOTS, :], identf[:, :]).then_inc(xT_ps, 1)

            def gates_by_position():
                pe.wait_ge(gate_oh_ready, 3)
                for n, (k, t) in enumerate((k, t) for k in range(2) for t in range(NT)):
                    last = pe.matmul(banks[3][:, 0:3 * RT], col_oh[:, k, t, :], gate_oh[:, k, t, :, :],
                                     start=(n == 0), stop=(n == 2 * NT - 1))
                last.then_inc(gates_ps, 1)

            def first_layer(s, w, hb):
                for c in range(HC):
                    last = pe.matmul(h_bank[hb][:, c * CAP:(c + 1) * CAP], w1_ring[:, s, c * P:(c + 1) * P], xT[:, w, :],
                                     start=True, stop=True)
                return last

            def second_layer(s, yb, slot):
                for c in range(HC):
                    last = pe.matmul(y_bank[yb][:, 0:CAP], w2_ring[:, s, c, :], hidden[:, slot, c, :],
                                     start=(c == 0), stop=(c == HC - 1))
                return last

            def rows(m, b, complete=None):
                n = rows_of_sorted(m)
                if complete is not None:
                    pe.wait_ge(yT_ready, complete)
                needs(pe, rows_ready, m - 1 if isinstance(m, int) and m > LEFT[0] else m)
                if isinstance(m, int):
                    src = yT_sorted[:, m * P:m * P + n]
                else:
                    pe.wait_ge(staged, m - STAGED0 + 1)
                    src = back_in[:, b, :]
                pe.transpose(back_bank[b][0:n, 0:D], src, identf[:, :]).then_inc(back_ps, 1)

            def slot(e, k):
                return slot_of(e) if isinstance(e, int) else k

            def step(e, k, it):
                if isinstance(e, int) and e == 0:
                    for m in range(tiles_ahead(-1)):
                        tokens(m)
                    gates_by_position()
                if not isinstance(e, int) or e < E:
                    if isinstance(e, int):
                        pe.wait_ge(w_in[slot_of(e) // 2], 32 * loads_in_slot(e))
                    else:
                        pe.wait_ge(w_in[k // 2], it * 32 + 32 * (loads_in_slot(2 * UNROLL + k) - 2))
                    needs(pe, hid_ready, 2 * (e - 1))
                    pe.wait_ge(window_ready, e + 1)
                    if isinstance(e, int) and e == 1:
                        pe.wait_ge(sorted_gate_ready, 1)
                    first_layer(slot(e, k), k % WINDOWS, k % 2).then_inc(h_ps, 1)
                if isinstance(e, int) and e == 2:
                    pe.wait_ge(bias_done, BIASED)
                if not isinstance(e, int) or e >= 2:
                    pe.wait_ge(hid_ready, 2 * (e - 1))
                    needs(pe, yT_ready, e - 3)
                    second_layer(slot(e - 2, (k - 2) % UNROLL), k % 2, (k - 2) % 4).then_inc(y_ps, 1)
                if isinstance(e, int) and e < 2 * UNROLL:
                    for m in range(tiles_ahead(e - 1), tiles_ahead(e)):
                        tokens(m)
                if flush := flush_tile(e, k, it):
                    rows(*flush, complete=e - 3)

            with pe.If(general > 0):
                for m in range(RT):
                    tokens(m)
                pe.wait_ge(bias_done, BIASED)
                gates_by_position()
                pe.wait_ge(sorted_gate_ready, 1)
                with pe.Fori(0, E // 2) as i:
                    for u in range(2):
                        wait_apart(pe, g_w_in[u], (i + 1) * 32)
                        with pe.Fori(0, WMAX) as w:
                            n = (i * 2 + u) * WMAX + w + 1
                            pe.wait_ge(g_window, n)
                            first_layer(u, 0, 0).then_inc(g_h_ps, 1)
                            pe.wait_ge(g_hid, n * 2)
                            second_layer(u, 0, 0).then_inc(g_y_ps, 1)
                        pe.wait_ge(g_yT, (i * 2 + u + 1) * WMAX + 1)
                        pe.sem_inc(g_w_free, 1)
                for m in range(RT):
                    rows(m, m % 2)
            with pe.Else():
                expert_steps(step)(pe)
                for m in LEFT:
                    rows(m, m % 2, E - 1 if m == LEFT[0] else E)

        @block.vector
        def _(dve):
            steps = Steps(dve, dve_link)
            link = steps.link

            def tile(buf, t, n):
                return buf[0:n, t, :] if isinstance(t, int) else buf[:, bass.ds(t, 1), :].rearrange("p o d -> p (o d)")

            dve.memset(mv[:, :, :], 1.0).then_inc(zeros_ready, 1)
            dve.memset(hx[:, NT - 1, :], 0.0).then_inc(zeros_ready, 1)
            dve.memset(hx[:, 0:NT - 1, D:D + 1], 1.0).then_inc(zeros_ready, 1)
            dve.memset(soft[:, :, N:NP], 0.0).then_inc(zeros_ready, 1)
            dve.wait_ge(zeros_ready, 4)
            dve.memset(hx[0:LAST, NT - 1, D:D + 1], 1.0).then_inc(zeros_ready, 1)

            def statistics(c):
                dve.wait_ge(x_in[c], 16 if c < NCH - 1 else 32)
                for t in chunk_tiles(c):
                    n = rows_of(t)
                    last = dve.bn_stats(bn[0:n, t, :], x_sb[0:n, t, :])
                link(last)
                for t in chunk_tiles(c):
                    n = rows_of(t)
                    last = dve.bn_aggr(mv[0:n, t, :], bn[0:n, t, :])
                last.then_inc(stats_ready, 1)

            def normalise(c):
                dve.wait_ge(rstd_ready, c + 1)
                for t in chunk_tiles(c):
                    n = rows_of(t)
                    last = dve.tensor_scalar(hx[0:n, t, 0:D], x_sb[0:n, t, :], mv[0:n, t, 0:1], rstd[0:n, t:t + 1],
                                             ALU.subtract, ALU.mult)
                last.then_inc(h_ready, 1)

            statistics(0)
            statistics(1)
            normalise(0)
            statistics(2)
            dve.wait_ge(a2_in, 16)
            dve.wait_ge(filled, 3)
            dve.tensor_scalar(a2_bc[:, :], ones_f[:, :], a2_sb[:, 0:1], ALPHA, ALU.mult, ALU.mult).then_inc(a2_ready, 1)
            normalise(1)
            normalise(2)
            dve.wait_ge(small_in, 16 * LOADS)
            dve.wait_ge(a1_in, 16)
            for t in range(NT):
                n = rows_of(t)
                dve.wait_ge(h_ready, t // TPC + 1)
                if t >= 2:
                    dve.wait_ge(w1_ready, t - 1)
                dve.tensor_tensor_reduce(out=w1_terms[0:n, t % 2, :], in0=hx[0:n, t, 0:D], in1=a1_bc[0:n, :], scale=1.0 - ALPHA,
                                         scalar=0.0, op0=ALU.mult, op1=ALU.add, accum_out=w1s[0:n, t:t + 1]).then_inc(w1_ready, 1)

            def logit_difference(part):
                ts = PARTS[part][0]
                dve.tensor_tensor(gden[:, ts], top8[:, ts, 1], top8[:, ts, 0], ALU.subtract).then_inc(diff_ready, 1)

            def gates(part, between):
                ts = PARTS[part][0]
                dve.wait_ge(gexp_ready, part + 1)
                n = steps.tick(dve.tensor_scalar(gden[:, ts], ge[:, ts], 1.0, None, ALU.add))
                between(0)
                steps.after(n)
                dve.reciprocal(gate[:, 0, ts], gden[:, ts]).then_inc(gates_ready, 1)
                between(1)
                dve.wait_ge(gates_ready, 2 * part + 1)
                dve.tensor_tensor(gate[:, 1, ts], ge[:, ts], gate[:, 0, ts], ALU.mult).then_inc(gates_ready, 1)

            def choose(ts):
                dve.wait_ge(const_made, 6)
                dve.wait_ge(logit_ready, ts.stop)
                for u in range(ts.start, ts.stop):
                    m = rows_of(u)
                    n = steps.tick(dve.max(top8[0:m, u, :], logit[0:m, u, :]))
                for u in range(ts.start, ts.stop):
                    m = rows_of(u)
                    steps.after(n - (ts.stop - 1 - u))
                    last = dve.max_index(idx8[0:m, u, :], top8[0:m, u, :], logit[0:m, u, :])
                link(last)
                m = rows_of(ts.stop - 1)
                link(dve.tensor_copy(exp2[0:m, :, ts], idx8[0:m, ts, 0:2].rearrange("p t k -> p k t")))
                g = ts.stop - ts.start
                for k in range(2):
                    ins = dve.tensor_tensor(oh[0:m, k, ts, :], iota_e[0:m, :].unsqueeze(1).to_broadcast([m, g, E]),
                                            exp2[0:m, k, ts].unsqueeze(2).to_broadcast([m, g, E]), ALU.is_equal)
                    steps.tick(ins)
                for k in range(2):
                    ins = dve.tensor_tensor(less[0:m, k, ts, :], iota_e[0:m, :].unsqueeze(1).to_broadcast([m, g, E]),
                                            exp2[0:m, k, ts].unsqueeze(2).to_broadcast([m, g, E]), ALU.is_gt)
                    if k == 0:
                        steps.tick(ins)
                    else:
                        ins.then_inc(oh_ready, g)

            def step(t, par):
                n = rows_of(t)
                q = (par + 1) % 2
                if isinstance(t, int) and t == NT + 1:
                    gates(0, lambda i: None)
                if has(t + 1):
                    m = rows_of(t + 1)
                    if isinstance(t, int) and t == -1:
                        dve.wait_ge(first_low, 1)
                    else:
                        dve.wait_ge(low_ready, t + 2)
                    dve.wait_ge(relu_ready, t + 2)
                    needs(dve, pT_ps, 3 * t)
                    if not isinstance(t, int):
                        dve.sem_inc(passed, 1)
                    dve.tensor_tensor_reduce(out=soft[0:m, q, 0:N], in0=relu_s[0:m, q, 0:N], in1=low[0:m, q, :],
                                             scale=-1.0, scalar=3e38, op0=ALU.add, op1=ALU.min,
                                             accum_out=zmin[0:m, q:q + 1]).then_inc(z_ready, 1)
                if has(t - 1):
                    u = rows_of(t - 1)
                    dve.wait_ge(o_ps, t)
                    divided = steps.tick(dve.reciprocal(rden[0:u, q:q + 1], o_bank[q][0:u, D:D + 1]))
                if has(t):
                    k = len(chunk_tiles(1))
                    dve.wait_ge(pT_ps, 3 * t + 2)
                    needs(dve, o_ps, t - 1)
                    dve.tensor_copy(pT[:, par, TPC:TPC + k, 0:n], tiles3(pt_bank[1], k, n)).then_inc(pT_dve, 1)
                if has(t - 1):
                    steps.after(divided)
                    summed = steps.tick(dve.scalar_tensor_tensor(tile(x1, t - 1, u), o_bank[q][0:u, 0:D], rden[0:u, q:q + 1],
                                                                 tile(x_sb, t - 1, u), ALU.mult, ALU.add))
                if has(t + 3):
                    m = rows_of(t + 3)
                    dve.wait_ge(adj_in[q], loads16(t + 3, q))
                    needs(dve, low_ready, t + 2)
                    dve.tensor_scalar(mask[0:m, q, :], adj_sb[0:m, q, :], 0.0, -BIG, ALU.is_le,
                                      ALU.mult).then_inc(mask_ready, 1)
                    if isinstance(t, int) and t == -2:
                        dve.wait_ge(mask_ready, 1)
                        for c in range(NCH):
                            js = slice(c * BANK, min((c + 1) * BANK, N))
                            dve.wait_ge(w2bc_ready, c + 1)
                            last = dve.tensor_tensor(low[:, 0, js], mask[:, 0, js], aw2_bc[:, js], ALU.add)
                        last.then_inc(first_low, 1)
                if has(t - 1):
                    steps.after(summed)
                    link(dve.bn_stats(bn2[0:u, q, :], tile(x1, t - 1, u)))
                    dve.bn_aggr(mv2[0:u, q, :], bn2[0:u, q, :]).then_inc(mv2_ready, 1)
                if has(t - 2):
                    m = rows_of(t - 2)
                    dve.wait_ge(logit_ps, t - 1)
                    dve.tensor_tensor(tile(logit, t - 2, m), c_bank[0:m, 0:E], br_bc[0:m, :], ALU.add).then_inc(logit_ready, 1)
                if has(t - 1):
                    if not isinstance(t, int) or t >= 3:
                        dve.wait_ge(xh2T_ps, t - 2)
                        dve.wait_ge(xh2_out[q], loads16(t - 3, q))
                    dve.wait_ge(rstd2_ready, t)
                    dve.tensor_scalar(xh2[0:u, q, :], tile(x1, t - 1, u), mv2[0:u, q, 0:1], rstd2[0:u, q:q + 1],
                                      ALU.subtract, ALU.mult).then_inc(xh2_ready, 1)
                if isinstance(t, int) and t in CHOICES:
                    choose(CHOICES[t])
                if isinstance(t, int) and t == NT:
                    dve.wait_ge(oh_ready, CHOICES[t].stop)
                    logit_difference(0)

            attention_steps(dve, step, steps)

            dve.wait_ge(oh_ready, NT)
            dve.wait_ge(const_made, CONST)
            logit_difference(1)
            dve.wait_ge(off_ps, 1)
            dve.tensor_copy(off_sb[:, :], off_bank[:, 0:E]).then_inc(off_ready, 1)
            dve.wait_ge(off_ready, 1)
            dve.wait_ge(rank_ps, 1)
            for bank, t0, t1 in rank_banks:
                link(dve.tensor_tensor(rowno[:, t0:t1, :], bank[:, 0:(t1 - t0) * E].rearrange("p (t e) -> p t e", e=E),
                                       off_sb[:, :].unsqueeze(1).to_broadcast([P, t1 - t0, E]), ALU.add))

            def pick(k):
                dve.tensor_tensor(picked[:, k, :, :], oh[:, k, :, :], rowno[:, :, :], ALU.mult).then_inc(picked_ready, 1)

            gates(1, pick)
            dve.wait_ge(picked_ready, 2)
            link(dve.tensor_reduce(pos[:, :, :], picked[:, :, :, :], AX_X, ALU.add))
            link(dve.tensor_tensor(pos_i[:, :, :], pos[:, :, :], nowhere[:, :, :], ALU.add))
            link(dve.tensor_scalar(pos_col[:, :, :], pos_i[:, :, :], P - 1, None, ALU.bitwise_and))
            dve.tensor_scalar(minus_col[:, :], pos_col[:, 1, :], -1.0, None, ALU.mult).then_inc(col_ready, 1)
            link(dve.tensor_scalar(pos_tile[:, :, :], pos_i[:, :, :], P.bit_length() - 1, None, ALU.logical_shift_right))
            dve.tensor_tensor(by_choice(tile_oh), iota_p[:, 0:RT].unsqueeze(1).to_broadcast([P, 2 * NT, RT]),
                              pos_tile[:, :, :].rearrange("p k t -> p (k t)").unsqueeze(2).to_broadcast([P, 2 * NT, RT]),
                              ALU.is_equal).then_inc(tile_oh_ready, 1)
            for k, n in ((0, NT), (1, NT - ACT_TILES)):
                dve.tensor_tensor(col_oh[:, k, 0:n, :], iota_p[:, :].unsqueeze(1).to_broadcast([P, n, P]),
                                  pos_col[:, k, 0:n].unsqueeze(2).to_broadcast([P, n, P]), ALU.is_equal
                                  ).then_inc(pos_oh_ready, 1)
                if k == 0:
                    dve.wait_ge(tile_oh_ready, 1)
                    dve.tensor_scalar(tok_oh[:, :, :, 0, :].rearrange("p k t m -> p (k t) m"), by_choice(tile_oh),
                                      tok_in_tile[:, 0:1], None, ALU.mult).then_inc(tok_oh_ready, 1)
            dve.wait_ge(guard_ready, 2)
            link(dve.tensor_reduce(most[:, :], guard[:, :], AX_X, ALU.max))
            dve.tensor_scalar(general_i[:, :], most[:, :], 0.0, None, ALU.is_gt).then_inc(general_ready, 1)
            dve.wait_ge(dst_ps, 1)
            link(dve.tensor_copy(dst_parts[:, :, :], c_bank[:, 0:2 * RT].rearrange("p (v m) -> p v m", v=2)))
            link(dve.tensor_tensor(dst_f[:, :], dst_parts[:, 0, :], dst_parts[:, 1, :], ALU.add))
            link(dve.tensor_scalar(second[:, :], dst_f[:, :], float(NP), -float(NP), ALU.is_ge, ALU.mult))
            dve.tensor_tensor(src_i[:, :], dst_f[:, :], second[:, :], ALU.add).then_inc(src_ready, 1)
            dve.tensor_copy(dst_i[:, :], dst_f[:, :]).then_inc(dst_ready, 1)
            general = take_general(dve)
            first = Positions(dve)
            dve.wait_ge(positions_ready, 2)
            first.load(last_off_i[0:1, 0:UNROLL])
            dve.wait_ge(gate_parts_ready, 1)
            for v in range(3):
                dve.tensor_tensor(gate_oh[:, :, :, v, :].rearrange("p k t m -> p (k t) m"), by_choice(tile_oh),
                                  gate_parts[:, v, :, :].rearrange("p k t -> p (k t)").unsqueeze(2).to_broadcast([P, 2 * NT, RT]),
                                  ALU.mult).then_inc(gate_oh_ready, 1)
            for c in range(NCH):
                dve.wait_ge(bias_ps, c + 1)
                ts = chunk_tiles(c)
                full = [t for t in ts if rows_of(t) == P]
                for t0, t1, m in [(full[0], full[-1] + 1, P)] + [(t, t + 1, LAST) for t in ts if t not in full]:
                    dve.tensor_tensor(x1[0:m, t0:t1, :], x1[0:m, t0:t1, :],
                                      bias_banks[c][0:m, (t0 - ts[0]) * D:(t1 - ts[0]) * D].rearrange("p (t d) -> p t d", d=D),
                                      ALU.add).then_inc(bias_done, 1)
            dve.wait_ge(gates_ps, 1)
            link(dve.tensor_copy(sorted_parts[:, :, :], banks[3][:, 0:3 * RT].rearrange("p (v m) -> p v m", v=3)))
            link(dve.tensor_tensor(sorted_gate[:, :], sorted_parts[:, 0, :], sorted_parts[:, 1, :], ALU.add))
            dve.tensor_tensor(sorted_gate[:, :], sorted_gate[:, :], sorted_parts[:, 2, :], ALU.add).then_inc(sorted_gate_ready, 1)
            dve.wait_ge(b1T_ready, 1)

            def bias_relu(e, hb, slot, done):
                for c in range(HC):
                    dve.tensor_scalar(hidden[:, slot, c, :], h_bank[hb][:, c * CAP:(c + 1) * CAP],
                                      b1T[:, c, bass.ds(e, 1)], 0.0, ALU.add, ALU.max).then_inc(done, 1)

            def step(e, k, it):
                if k == 0 and not (isinstance(e, int) and e == 0):
                    n = 2 if isinstance(e, int) and e == E else UNROLL
                    first.load(last_off_i[0:1, bass.ds(e, n)], n)
                if not isinstance(e, int) or e < E:
                    needs(dve, y_ps, e - 3)
                    dve.wait_ge(h_ps, e + 1)
                    bias_relu(e, k % 2, k % 4, hid_ready)
                if not isinstance(e, int) or e >= 2:
                    needs(dve, yT_ready, e - 2)
                    wait_apart(dve, y_ps, e - 1)
                    dve.tensor_copy(yT_sorted[:, bass.ds(first[k], CAP)], y_bank[k % 2][:, 0:CAP]).then_inc(yT_ready, 1)
                if not isinstance(e, int) and (flush := flush_tile(e + 2, k + 2, it)):
                    m, b = flush
                    dve.wait_ge(back_ps, m)
                    wait_apart(dve, yT_ready, e - 1)
                    dve.tensor_copy(back_in[:, b, :], yT_sorted[:, bass.ds(m * P, P)]).then_inc(staged, 1)

            dve.wait_ge(positions_ready, 2)
            with dve.If(general > 0):
                for w in range(WMAX):
                    at = window_at[:, :, w]
                    dve.scalar_tensor_tensor(at, offs[:, 0:E], float(CAP * w), offs[:, 1:E + 1], ALU.add,
                                             ALU.min).then_inc(windows_made, 1)
                dve.wait_ge(windows_made, WMAX)
                dve.tensor_copy(window_i[:, :], window_at[:, :, :].rearrange("p e w -> p (e w)")).then_inc(windows_ready, 1)
                with dve.Fori(0, E) as e:
                    with dve.Fori(0, WMAX) as w:
                        n = e * WMAX + w + 1
                        dve.wait_ge(g_h_ps, n)
                        bias_relu(e, 0, 0, g_hid)
                        at = dve.value_load(window_i[0:1, bass.ds(e * WMAX + w, 1)], min_val=0, max_val=R)
                        wait_apart(dve, g_y_ps, n)
                        dve.tensor_copy(yT_sorted[:, bass.ds(at, CAP)], y_bank[0][:, 0:CAP]).then_inc(g_yT, 1)
            with dve.Else():
                expert_steps(step)(dve)
            for g, (t0, t1) in enumerate(SUMS):
                dve.wait_ge(y2_in[g], 32)
                m = rows_of(t0)
                if g == 0:
                    dve.wait_ge(bias_done, BIASED)
                if g == POOL_SUM:
                    continue
                rows = x1[0:m, t0:t1, :]
                link(dve.tensor_tensor(rows, rows, y2[0:m, 0, t0:t1, :], ALU.add))
                dve.tensor_tensor(rows, rows, y2[0:m, 1, t0:t1, :], ALU.add).then_inc(sums_done[g], 1)


_INS = ['x', 'adj', 'L0_gnn_a', 'L0_ffn_Wr', 'L0_ffn_br', 'L0_ffn_W1', 'L0_ffn_b1', 'L0_ffn_W2', 'L0_ffn_b2']


def kernel(**inputs):
    import numpy as _np
    import concourse.bacc as _bacc
    from concourse import mybir as _mybir
    from concourse.bass_utils import run_bass_kernel_spmd as _run

    nc = _bacc.Bacc("TRN2", target_bir_lowering=False, num_devices=1)
    arrays, args = {}, []
    for name in _INS:
        v = _np.ascontiguousarray(inputs[name])
        arrays[f"in_{name}_dram"] = v
        args.append(nc.dram_tensor(f"in_{name}_dram", v.shape, _mybir.dt.from_np(v.dtype), kind="ExternalInput").ap())
    shape = tuple(inputs["x"].shape)
    args.append(nc.dram_tensor("out_0_dram", shape, _mybir.dt.float32, kind="ExternalOutput").ap())
    gat_moe(nc, *args)
    r = _run(nc, [arrays], core_ids=[0])
    return r.results[0]["out_0_dram"]
```
